# Optimizing a Trainium2 kernel written in Bass

```python
import numpy as np
import jax
import jax.numpy as jnp

def _softmax(x, axis=-1):
    return jax.nn.softmax(x, axis=axis)

def _gelu(x):
    return jax.nn.gelu(x, approximate=True)

def _silu(x):
    return jax.nn.silu(x)

def _sigmoid(x):
    return jax.nn.sigmoid(x)

def _layernorm(x, axis=-1, eps=1e-05):
    m = jnp.mean(x, axis=axis, keepdims=True)
    v = jnp.var(x, axis=axis, keepdims=True)
    return (x - m) / jnp.sqrt(v + eps)

def _scatter_add(tgt, idx, src, axis=0):
    return tgt.at[idx].add(src)

def _segment_sum(src, seg, n):
    return jax.ops.segment_sum(src, seg, n)
kernel_name = 'mk_cond_resid_d2_seqx_r4_6ac598'

def setup_inputs(seed: int=0):
    np.random.seed(seed)
    _w = jnp.asarray

    def _rec_inputs():
        import jax
        import jax.numpy as jnp
        _rk = jax.random.key(seed)
        x = 7.22e-05 + 1 * jax.random.normal(jax.random.fold_in(_rk, 1), (16, 256, 512), jnp.float32)
        _lenS = 256 - jax.random.randint(jax.random.fold_in(_rk, 7), (16,), 0, max(1, 256 // 4) + 1, jnp.int32)
        _lenS2 = 256 - jax.random.randint(jax.random.fold_in(_rk, 8), (16,), 0, max(1, 256 // 4) + 1, jnp.int32)
        cond_2048 = jax.random.bernoulli(jax.random.fold_in(_rk, 11), 0.5063, (16, 512)).astype(jnp.float32)
        return (x, cond_2048)
    x, cond_2048 = _rec_inputs()

    def _L0_cond_setup():
        import jax, jax.numpy as jnp
        import numpy as np
        NH = 8
        NEG = -1e+30
        key = jax.random.key(seed)
        k1, k2, k3, k4 = jax.random.split(key, 4)
        B, D, T = (4, 256, 512)
        x = jax.random.normal(k1, (B, D, T), dtype=jnp.float32)
        mask = jax.random.randint(k2, (B, T), 0, 2).astype(jnp.float32)
        lim = float(np.sqrt(6.0 / (D + D)))
        Wq = jax.random.uniform(k3, (D, D), dtype=jnp.float32, minval=-lim, maxval=lim)
        Wo = jax.random.uniform(k4, (D, D), dtype=jnp.float32, minval=-lim, maxval=lim)
        return {'x': x, 'mask': mask, 'Wq': Wq, 'Wo': Wo}
    _L0_cond_all = _L0_cond_setup()
    _L0_cond_in = {k: v for k, v in _L0_cond_all.items() if k in ('Wq', 'Wo')}
    del _L0_cond_all

    def _L1_cond_setup():
        import jax, jax.numpy as jnp
        import numpy as np
        B, T, D = (16, 128, 512)
        key = jax.random.key(seed)
        k0, k1, k2, k3 = jax.random.split(key, 4)
        scale = 1.0 / np.sqrt(D)
        return {'initial_state': jax.random.normal(k0, (B, D), jnp.float32), 'inputs': jax.random.normal(k1, (B, T, D), jnp.float32), 'W_ih': jax.random.normal(k2, (D, 3 * D), jnp.float32) * scale, 'W_hh': jax.random.normal(k3, (D, 3 * D), jnp.float32) * scale, 'b_ih': jnp.zeros((3 * D,), jnp.float32), 'b_hh': jnp.zeros((3 * D,), jnp.float32)}
    _L1_cond_all = _L1_cond_setup()
    _L1_cond_in = {k: v for k, v in _L1_cond_all.items() if k in ('W_ih', 'W_hh', 'b_ih', 'b_hh')}
    del _L1_cond_all
    return {'x': x, 'cond_2048': cond_2048, 'L0_cond_Wq': _L0_cond_in['Wq'], 'L0_cond_Wo': _L0_cond_in['Wo'], 'L1_cond_W_ih': _L1_cond_in['W_ih'], 'L1_cond_W_hh': _L1_cond_in['W_hh'], 'L1_cond_b_ih': _L1_cond_in['b_ih'], 'L1_cond_b_hh': _L1_cond_in['b_hh']}

def reference(x, cond_2048, L0_cond_Wq, L0_cond_Wo, L1_cond_W_ih, L1_cond_W_hh, L1_cond_b_ih, L1_cond_b_hh):
    import jax
    import jax.numpy as jnp

    def _L0_cond_ref(x, mask, Wq, Wo):
        import jax, jax.numpy as jnp
        import numpy as np
        NH = 8
        NEG = -1e+30
        B, D, T = x.shape
        dk = D // NH
        scale = 1.0 / jnp.sqrt(jnp.asarray(dk, x.dtype))
        xt = jnp.transpose(x, (0, 2, 1))
        q = xt @ Wq.T
        qh = q.reshape(B, T, NH, dk).transpose(0, 2, 1, 3)
        scores = scale * jnp.einsum('bhqd,bhkd->bhqk', qh, qh)
        cmask = mask[:, None, None, :]
        rmask = mask[:, None, :, None]
        logits = (scores * cmask + (1.0 - cmask) * NEG) * rmask
        attn = jax.nn.softmax(logits, axis=-1)
        ctx = jnp.einsum('bhqk,bhkd->bhqd', attn, qh)
        ctx = ctx.transpose(0, 2, 1, 3).reshape(B, T, D)
        out = ctx @ Wo.T
        return jnp.transpose(out, (0, 2, 1))

    def _L1_cond_ref(initial_state, inputs, W_ih, W_hh, b_ih, b_hh):
        import jax, jax.numpy as jnp
        import numpy as np
        B, T, D = (16, 128, 512)
        "ScanOverTime(GRU cell): sequential per-timestep module call with\n            dict-state passing; merge_dict_trees stacks the per-step\n            'state_predicted' tensors along axis=1 -> [B, T, D]."

        def cell(h, x):
            gi = x @ W_ih + b_ih
            gh = h @ W_hh + b_hh
            i_r, i_z, i_n = jnp.split(gi, 3, axis=-1)
            h_r, h_z, h_n = jnp.split(gh, 3, axis=-1)
            r = jax.nn.sigmoid(i_r + h_r)
            z = jax.nn.sigmoid(i_z + h_z)
            n = jnp.tanh(i_n + r * h_n)
            h_new = (1.0 - z) * n + z * h
            return (h_new, h_new)
        xs = jnp.swapaxes(inputs, 0, 1)
        _, hs = jax.lax.scan(cell, initial_state, xs)
        return jnp.swapaxes(hs, 0, 1)
    x = x + _L0_cond_ref(x, cond_2048, L0_cond_Wq, L0_cond_Wo)
    x = x + _L1_cond_ref(cond_2048, x, L1_cond_W_ih, L1_cond_W_hh, L1_cond_b_ih, L1_cond_b_hh)
    return x

_drawn_inputs = setup_inputs


def setup_inputs(seed=0):
    import zlib

    import numpy as np

    out = dict(_drawn_inputs(seed))
    spreads = {'L1_cond_b_ih': (0.0, 0.1), 'L1_cond_b_hh': (0.0, 0.1)}
    factors = {}
    for name, (base, spread) in spreads.items():
        noise = np.random.default_rng([zlib.crc32(name.encode()), seed]).standard_normal(out[name].shape)
        drawn = base * np.exp(spread * noise) if base else spread * noise
        out[name] = jnp.asarray(drawn.astype(out[name].dtype))
    for name, factor in factors.items():
        out[name] = (out[name] * factor).astype(out[name].dtype)
    return out
```

```python
from contextlib import ExitStack

import concourse.bass as bass
from concourse import mybir

F32 = mybir.dt.float32
BF16 = mybir.dt.bfloat16
ALU = mybir.AluOpType
ACT = mybir.ActivationFunctionType
AX = mybir.AxisListType

P = 128
B = 16
D = 256
T = 512
NH = 8
DK = D // NH
HG = P // DK
NG = NH // HG
GROUPS = B * NG
KT = T // P
TILES = KT * HG
BIG = 1e30
SCALE = DK ** -0.5
PASS2 = 2 * DK + 2 * KT + 1
P_RING = 2

KF = T // P
CH = 8
CHUNKS = D // CH
CB = CH * B
FILL = 7
EVAC = [3, 5, 7]
GATES = 3


STACKED = 16 * (12 * HG + 2)
PLACED = 16 * 2 * HG


def wait(eng, sem, value):
    if not isinstance(value, int) or value > 0:
        eng.wait_ge(sem, value)


def early(eng, value):
    return value if isinstance(value, int) else eng.compute_val(value)


def attention(nc, ctx, io, xT, ident):
    def sb(name, shape, dt=F32):
        return ctx.enter_context(nc.sbuf_tensor(name, shape, dt))

    def ps(name):
        return ctx.enter_context(nc.psum_tensor(name, [P, 512], F32))

    def sem(name):
        return ctx.enter_context(nc.semaphore(name))

    wq = sb("wq", [P, NG, D])
    wo = sb("wo", [P, NG, D])
    x_proj = sb("x_proj", [P, NG, T])
    x_res = sb("x_res", [P, NG, T])
    mask_cols = sb("mask_cols", [P, T])
    mask_rows = sb("mask_rows", [B, T])
    live = sb("live", [B, T], BF16)
    dead = sb("dead", [B, T], BF16)
    q_all = sb("q_all", [P, T])
    q_live = sb("q_live", [P, T])
    q_rest = sb("q_rest", [P, T])
    q_hi = sb("q_hi", [P, T], BF16)
    q_mid = sb("q_mid", [P, T], BF16)
    q_lo = sb("q_lo", [P, T], BF16)
    keys1 = [sb(f"keys1_{p}", [P, HG, T], BF16) for p in range(2)]
    qrys1 = [sb(f"qrys1_{p}", [P, HG, T], BF16) for p in range(2)]
    keys2 = [sb(f"keys2_{p}", [P, HG, T], BF16) for p in range(2)]
    qrys2 = [sb(f"qrys2_{p}", [P, HG, T], BF16) for p in range(2)]
    vals = [sb(f"vals_{p}", [P, KT, P]) for p in range(2)]
    probs = sb("probs", [P, P_RING, HG, T])
    row_max = sb("row_max", [P, HG * KT])
    diag = sb("diag", [HG * KT, KT, P])
    max_rows = sb("max_rows", [HG * KT, KT, P])
    max_hi = sb("max_hi", [HG * KT, KT, P], BF16)
    max_lo = sb("max_lo", [HG * KT, KT, P], BF16)
    ones = sb("ones", [P, DK])
    sums = sb("sums", [P, T])
    raw = sb("raw", [P, T])
    inv_sum = sb("inv_sum", [P, T])
    context = [sb(f"context_{g}", [P, T]) for g in range(NG)]

    peek = [ps(f"peek_{i}") for i in range(2)]
    score = [ps(f"score_{i}") for i in range(2)]
    pv = ps("pv")
    psum_p = ps("psum_p")
    small = ps("small")
    final = ps("final")

    const_in, x_in, mask_in, xres_in = sem("const_in"), sem("x_in"), sem("mask_in"), sem("xres_in")
    mrow_in, live_made, dead_made, mrow_out = sem("mrow_in"), sem("live_made"), sem("dead_made"), sem("mrow_out")
    ones_made = sem("ones_made")
    q_done, q_copied, q_masked = sem("q_done"), sem("q_copied"), sem("q_masked")
    hi_made, rest_made, mid_made, lo_made, rest2_made = (sem("hi_made"), sem("rest_made"), sem("mid_made"),
                                                         sem("lo_made"), sem("rest2_made"))
    stacked = sem("stacked")
    v_turned, v_copied = sem("v_turned"), sem("v_copied")
    peek_done, peek_used = sem("peek_done"), sem("peek_used")
    max_turned, max_spread, maxhi_made, maxlo_made, max_in = (sem("max_turned"), sem("max_spread"),
                                                              sem("maxhi_made"), sem("maxlo_made"), sem("max_in"))
    score_done, probs_made = sem("score_done"), sem("probs_made")
    round_done, inv_made, context_made = sem("round_done"), sem("inv_made"), sem("context_made")
    sums_copied = sem("sums_copied")
    final_done, final_used = sem("final_done"), sem("final_used")

    x_d = io["x"].rearrange("b (g p) t -> b p g t", p=P)

    def next_group(b, g, n=1):
        return (b, g + n) if g + n < NG else (b + (g + n) // NG, (g + n) % NG)

    def exists(b):
        return not isinstance(b, int) or 0 <= b < B

    def number(b, g):
        return b * NG + g

    block = ctx.enter_context(nc.Block())

    def staged(eng, stage):
        stage(-1, 0)
        stage(-1, 1)
        stage(0, 0)
        stage(0, 1)
        with eng.Fori(1, B - 1) as b:
            for g in range(NG):
                stage(b, g)
        stage(B - 1, 0)
        stage(B - 1, 1)
        stage(B, 0)

    @block.sync
    def _(sp):
        sp.dma_start(wq[:, :, :], io["wq"].rearrange("(g p) n -> p g n", p=P)).then_inc(const_in, 16)
        sp.dma_start(wo[:, :, :], io["wo"].rearrange("(g p) n -> p g n", p=P)).then_inc(const_in, 16)
        sp.dma_start(ident[:, :], io["ident"]).then_inc(const_in, 16)
        sp.dma_start(diag[:, :, :], io["diag"].rearrange("r (a c) -> r a c", a=KT)).then_inc(const_in, 16)

        def load_x(b):
            wait(sp, q_done, number(b, 0))
            sp.dma_start(x_proj[:, :, :], x_d[b]).then_inc(x_in, 16)
            wait(sp, q_masked, number(b, 0))
            sp.dma_start(mask_cols[:, :], io["mask"][bass.ds(b, 1), :].partition_broadcast(P)).then_inc(mask_in, 16)

        def stack(b, g):
            n = number(b, g)
            made_at, read_at = early(sp, n + 1), early(sp, TILES * (n - 1))
            wait(sp, score_done, read_at)
            for part, made, places in (
                (q_hi, hi_made, ((keys1, 0), (qrys1, 0), (qrys1, 1), (keys1, 2), (qrys1, 3), (keys2, 0))),
                (q_mid, mid_made, ((keys1, 1), (qrys1, 2), (keys2, 1), (qrys2, 1))),
                (q_lo, lo_made, ((keys1, 3), (qrys2, 0))),
            ):
                sp.wait_ge(made, made_at)
                for buffers, quarter in places:
                    for h in range(HG):
                        sp.dma_start(buffers[g][DK * quarter:DK * quarter + DK, h, :],
                                     part[DK * h:DK * h + DK, :]).then_inc(stacked, 16)
            at = 2 * DK + 2 * KT
            for buffers, row in ((keys2, "dead"), (qrys2, "live")):
                sp.dma_start(buffers[g][at:at + 1, :, :],
                             io[row][bass.ds(b, 1), :].rearrange("o (h t) -> o h t", h=1)
                             .to_broadcast([1, HG, T])).then_inc(stacked, 16)

        def place_max(b, g):
            n = number(b, g)
            for part, made, at in ((max_hi, maxhi_made, 2 * DK), (max_lo, maxlo_made, 2 * DK + KT)):
                sp.wait_ge(made, n + 1)
                for h in range(HG):
                    sp.dma_start(qrys2[g][at:at + KT, h, :],
                                 part[KT * h:KT * h + KT, :, :].rearrange("p a c -> p (a c)")).then_inc(max_in, 16)

        def stage(b, g):
            b1, g1 = next_group(b, g)
            b2, g2 = next_group(b, g, 2)
            if exists(b1):
                stack(b1, g1)
            if g2 == 0 and exists(b2):
                load_x(b2)
            if g == NG - 1 and exists(b):
                wait(sp, final_done, 2 * b)
                sp.dma_start(x_res[:, :, :], x_d[b]).then_inc(xres_in, 16)
            if exists(b1):
                place_max(b1, g1)

        sp.wait_ge(mrow_out, 32)
        sp.wait_ge(ones_made, 5)
        staged(sp, stage)

    @block.gpsimd
    def _(pool):
        for buf in (*keys2, *qrys2):
            pool.memset(buf[2 * DK:PASS2 + 23, :, :], 1.0).then_inc(ones_made, 1)
        pool.wait_ge(ones_made, len(keys2) + len(qrys2))
        pool.memset(ones[:, :], 1.0).then_inc(ones_made, 1)
        pool.dma_start(mask_rows[:, :], io["mask"]).then_inc(mrow_in, 16)
        pool.wait_ge(live_made, 1)
        pool.dma_start(io["live"], live[:, :]).then_inc(mrow_out, 16)
        pool.wait_ge(dead_made, 2)
        pool.dma_start(io["dead"], dead[:, :]).then_inc(mrow_out, 16)

        def stage(b, g):
            b2, g2 = next_group(b, g, 2)
            if not exists(b2):
                return
            n = number(b2, g2)
            pool.wait_ge(mid_made, n + 1)
            wait(pool, stacked, STACKED * n)
            pool.tensor_tensor(q_lo[:, :], q_rest[:, :], q_mid[:, :], ALU.subtract).then_inc(lo_made, 1)

        staged(pool, stage)

    @block.scalar
    def _(act):
        def project(b, g):
            n = number(b, g)
            act.wait_ge(q_masked, n + 1)
            wait(act, v_turned, n)
            act.activation(q_all[:, :], small[:, :], ACT.Copy).then_inc(q_copied, 1)
            wait(act, stacked, STACKED * n)
            act.activation(q_hi[:, :], q_live[:, :], ACT.Copy).then_inc(hi_made, 1)
            act.wait_ge(rest_made, n + 1)
            act.activation(q_mid[:, :], q_rest[:, :], ACT.Copy).then_inc(mid_made, 1)

        def values(b, g):
            n = number(b, g)
            act.wait_ge(v_turned, n + 1)
            wait(act, round_done, KT * (n - 1))
            act.activation(vals[g][:, :, :].rearrange("p a c -> p (a c)"), small[:, :],
                           ACT.Copy).then_inc(v_copied, 1)

        def finish(b):
            for half in range(2):
                act.wait_ge(final_done, 2 * b + half + 1)
                act.activation(xT[:, 2 * half:2 * half + 2, :, bass.ds(b, 1)].rearrange("p k t o -> p k (t o)"),
                               final[:, :].rearrange("p (k t) -> p k t", k=2), ACT.Copy).then_inc(final_used, 1)

        def stage(b, g):
            b1, g1 = next_group(b, g)
            b2, g2 = next_group(b, g, 2)
            n = number(b, g)
            for i in range(KT):
                if exists(b):
                    for h in range(HG):
                        act.wait_ge(score_done, TILES * n + HG * i + h + 1)
                        if h == 0 and (not isinstance(b, int) or KT * n + i >= P_RING):
                            act.wait_ge(round_done, KT * n + i - P_RING + 1)
                        act.activation(probs[:, i % P_RING, h, :], score[h % 2][:, :], ACT.Exp,
                                       scale=SCALE).then_inc(probs_made, 1)
                if i == 1 and exists(b1):
                    values(b1, g1)
                if i == 2 and g == 0 and exists(b - 1):
                    finish(b - 1)
            if exists(b2):
                project(b2, g2)

        staged(act, stage)

    @block.vector
    def _(dve):
        dve.wait_ge(mrow_in, 16)
        dve.tensor_copy(live[:, :], mask_rows[:, :]).then_inc(live_made, 1)
        dve.tensor_scalar(mask_rows[:, :], mask_rows[:, :], -1.0, None, ALU.add).then_inc(dead_made, 1)
        dve.wait_ge(dead_made, 1)
        dve.tensor_scalar(dead[:, :], mask_rows[:, :], BIG, None, ALU.mult).then_inc(dead_made, 1)

        def project(b, g):
            n = number(b, g)
            dve.wait_ge(q_done, n + 1)
            dve.wait_ge(mask_in, 16 * (b + 1))
            wait(dve, hi_made, n)
            dve.tensor_tensor(q_live[:, :], small[:, :], mask_cols[:, :], ALU.mult).then_inc(q_masked, 1)
            dve.wait_ge(hi_made, n + 1)
            dve.wait_ge(q_masked, n + 1)
            wait(dve, lo_made, n)
            dve.tensor_tensor(q_rest[:, :], q_live[:, :], q_hi[:, :], ALU.subtract).then_inc(rest_made, 1)

        def maxima(b, g):
            n = number(b, g)
            wait(dve, max_turned, n)
            for i in range(KT):
                for h in range(HG):
                    dve.wait_ge(peek_done, TILES * n + HG * i + h + 1)
                    dve.tensor_reduce(row_max[:, KT * h + i:KT * h + i + 1], peek[h % 2][:, :], AX.X,
                                      ALU.max).then_inc(peek_used, 1)

        def spread(b, g):
            n = number(b, g)
            dve.wait_ge(max_turned, n + 1)
            turned = small[0:HG * KT, 0:P].rearrange("r (o c) -> r o c", o=1).to_broadcast([HG * KT, KT, P])
            dve.tensor_tensor(max_rows[:, :, :], turned, diag[:, :, :], ALU.mult).then_inc(max_spread, 1)
            dve.wait_ge(max_spread, n + 1)
            wait(dve, max_in, PLACED * n)
            dve.tensor_copy(max_hi[:, :, :], max_rows[:, :, :]).then_inc(maxhi_made, 1)
            dve.wait_ge(maxhi_made, n + 1)
            dve.tensor_tensor(max_lo[:, :, :], max_rows[:, :, :], max_hi[:, :, :],
                              ALU.subtract).then_inc(maxlo_made, 1)

        def normalise(b, g):
            n = number(b, g)
            dve.wait_ge(round_done, KT * (n + 1))
            dve.tensor_copy(sums[:, :], psum_p[:, :]).then_inc(sums_copied, 1)
            wait(dve, context_made, n)
            dve.tensor_copy(raw[:, :], pv[:, :]).then_inc(sums_copied, 1)
            dve.wait_ge(sums_copied, 2 * n + 2)
            dve.reciprocal(inv_sum[:, :], sums[:, :]).then_inc(inv_made, 1)
            dve.wait_ge(inv_made, n + 1)
            if not isinstance(b, int) or b >= 1:
                dve.wait_ge(final_done, 2 * b)
            dve.tensor_tensor(context[g][:, :], raw[:, :], inv_sum[:, :], ALU.mult).then_inc(context_made, 1)

        def stage(b, g):
            b0, g0 = (b, g - 1) if g else (b - 1, NG - 1)
            b1, g1 = next_group(b, g)
            b2, g2 = next_group(b, g, 2)
            if exists(b0):
                normalise(b0, g0)
            if exists(b1):
                maxima(b1, g1)
            if exists(b2):
                project(b2, g2)
            if exists(b1):
                spread(b1, g1)

        dve.wait_ge(const_in, 64)
        staged(dve, stage)

    @block.tensor
    def _(pe):
        pe.wait_ge(const_in, 64)
        pe.wait_ge(ones_made, 5)

        def project(b, g):
            n = number(b, g)
            pe.wait_ge(x_in, 16 * (b + 1))
            wait(pe, v_copied, n)
            for k in range(NG):
                mm = pe.matmul(small[:, :], wq[:, k, P * g:P * g + P], x_proj[:, k, :],
                               start=(k == 0), stop=(k == NG - 1))
            mm.then_inc(q_done, 1)

        def peeks(b, g, i):
            n = number(b, g)
            if i == 0:
                pe.wait_ge(stacked, STACKED * (n + 1))
            for h in range(HG):
                wait(pe, peek_used, TILES * n + HG * i + h - 1)
                pe.matmul(peek[h % 2][:, :], keys1[g][:, h, P * i:P * i + P], qrys1[g][:, h, :],
                          start=True, stop=True).then_inc(peek_done, 1)

        def turn_max(b, g):
            n = number(b, g)
            pe.wait_ge(peek_used, TILES * (n + 1))
            wait_projected(b, g)
            pe.transpose(small[0:HG * KT, 0:P], row_max[:, :], ident[:, :]).then_inc(max_turned, 1)

        def wait_projected(b, g):
            b2, g2 = next_group(b, g)
            n2 = number(b2, g2) if exists(b2) else GROUPS - 1
            pe.wait_ge(q_copied, n2 + 1)
            pe.wait_ge(q_masked, n2 + 1)

        def turn_values(b, g):
            n = number(b, g)
            pe.wait_ge(q_copied, n + 1)
            pe.wait_ge(q_masked, n + 1)
            wait(pe, max_spread, n)
            for a in range(KT):
                mm = pe.transpose(small[:, P * a:P * a + P], q_all[:, P * a:P * a + P], ident[:, :])
            mm.then_inc(v_turned, 1)

        def scores(b, g, i):
            n = number(b, g)
            if i == 0:
                pe.wait_ge(max_in, PLACED * (n + 1))
            for h in range(HG):
                wait(pe, probs_made, TILES * n + HG * i + h - 1)
                pe.matmul(score[h % 2][:, :], keys1[g][:, h, P * i:P * i + P], qrys1[g][:, h, :],
                          start=True, stop=False)
                pe.matmul(score[h % 2][:, :], keys2[g][0:PASS2, h, P * i:P * i + P], qrys2[g][0:PASS2, h, :],
                          start=False, stop=True).then_inc(score_done, 1)

        def weigh(b, g, i):
            n = number(b, g)
            if i == 0:
                wait(pe, sums_copied, 2 * n)
                pe.wait_ge(v_copied, n + 1)
            pe.wait_ge(probs_made, TILES * n + HG * (i + 1))
            for h in range(HG):
                pe.matmul(pv[DK * h:DK * h + DK, :], vals[g][:, i, DK * h:DK * h + DK], probs[:, i % P_RING, h, :],
                          start=(i == 0), stop=(i == KT - 1))
            for h in range(HG):
                mm = pe.matmul(psum_p[DK * h:DK * h + DK, :], ones[:, :], probs[:, i % P_RING, h, :],
                               start=(i == 0), stop=(i == KT - 1))
            mm.then_inc(round_done, 1)

        def finish(b):
            pe.wait_ge(context_made, NG * (b + 1))
            pe.wait_ge(xres_in, 16 * (b + 1))
            for half in range(2):
                wait(pe, final_used, 2 * b + half)
                for kk in range(2):
                    k = 2 * half + kk
                    at = D * kk
                    for g in range(NG):
                        pe.matmul(final[:, at + P * g:at + P * g + P], x_res[:, g, P * k:P * k + P], ident[:, :],
                                  start=(kk == 0 and g == 0), stop=False, is_transpose=True, skip_group_check=True)
                    for g in range(NG):
                        mm = pe.matmul(final[:, at:at + D], context[g][:, P * k:P * k + P], wo[:, g, :],
                                       start=False, stop=(g == NG - 1), skip_group_check=True)
                mm.then_inc(final_done, 1)

        def stage(b, g):
            b0, g0 = (b, g - 1) if g else (b - 1, NG - 1)
            b1, g1 = next_group(b, g)
            b2, g2 = next_group(b, g, 2)
            for i in range(KT):
                if exists(b):
                    scores(b, g, i)
                if i == 0 and exists(b0):
                    weigh(b0, g0, KT - 1)
                if i >= 1 and exists(b):
                    weigh(b, g, i - 1)
                if exists(b1):
                    peeks(b1, g1, i)
                if i == 0 and exists(b1):
                    turn_values(b1, g1)
                if i == 2 and g == 0 and exists(b0):
                    finish(b0)
            if exists(b2):
                project(b2, g2)
            if exists(b1):
                turn_max(b1, g1)

        staged(pe, stage)


def gru(nc, ctx, io, xT, ident):
    def sb(name, shape, dt=F32):
        return ctx.enter_context(nc.sbuf_tensor(name, shape, dt))

    def ps(name):
        return ctx.enter_context(nc.psum_tensor(name, [P, 512], F32))

    def sem(name):
        return ctx.enter_context(nc.semaphore(name))

    whh = sb("whh", [P, KF, KF, GATES * P])
    wih = sb("wih", [P, KF, GATES * T])
    bias_i = sb("bias_i", [P, GATES * KF])
    bias_h = sb("bias_h", [P, GATES * KF])
    state = [sb(f"state_{c}", [P, KF, CH, B]) for c in range(2)]
    cond = sb("cond", [P, P])
    xc = [sb(f"xc_{c}", [P, KF, CB]) for c in range(2)]
    gi = [sb(f"gi_{c}", [P, GATES, KF, CH, B]) for c in range(2)]
    sum_rn = sb("sum_rn", [P, 2 * P])
    sum_z = sb("sum_z", [P, P])
    r_pre, r_gate, hn, rhn, n_pre, n_gate, z_pre, z_gate, diff, zdiff = (
        sb(name, [P, KF, B]) for name in ("r_pre", "r_gate", "hn", "rhn", "n_pre", "n_gate",
                                          "z_pre", "z_gate", "diff", "zdiff"))
    y = sb("y", [P, KF, CB])
    y_rows = sb("y_rows", [P, T])

    rn = ps("rn")
    z = ps("z")
    rn_turned = ps("rn_turned")
    z_turned = ps("z_turned")
    gi_sum = [ps(f"gi_sum_{q}") for q in range(GATES)]
    y_turned = ps("y_turned")

    w_in, whh_in, cond_in, b_made, zeroed, psum_zeroed = (sem("w_in"), sem("whh_in"), sem("cond_in"), sem("b_made"),
                                                          sem("zeroed"), sem("psum_zeroed"))
    h0_turned, state_made = sem("h0_turned"), sem("state_made")
    xc_made, gi_summed, gi_made = sem("xc_made"), sem("gi_summed"), sem("gi_made")
    rn_done, z_done, rn_copied, z_copied, rnT_done, zT_done = (
        sem("rn_done"), sem("z_done"), sem("rn_copied"), sem("z_copied"), sem("rnT_done"), sem("zT_done"))
    rpre_made, hn_made, r_made, rhn_made, npre_made, n_made = (
        sem("rpre_made"), sem("hn_made"), sem("r_made"), sem("rhn_made"), sem("npre_made"), sem("n_made"))
    zpre_made, z_made, diff_made, zdiff_made = sem("zpre_made"), sem("z_made"), sem("diff_made"), sem("zdiff_made")
    y_made, y_done, y_copied, y_out = sem("y_made"), sem("y_done"), sem("y_copied"), sem("y_out")

    out_d = io["out"].rearrange("b t f -> t b f")

    block = ctx.enter_context(nc.Block())

    def chunked(eng, chunk):
        chunk(0, 0)
        chunk(1, 1)
        with eng.Fori(1, CHUNKS // 2 - 1) as pair:
            chunk(2 * pair, 0)
            chunk(2 * pair + 1, 1)
        chunk(CHUNKS - 2, 0)
        chunk(CHUNKS - 1, 1)

    def is_first(c):
        return isinstance(c, int) and c == 0

    def is_last(c):
        return isinstance(c, int) and c == CHUNKS - 1

    def turned(psum, at):
        return psum[:, at:at + P].rearrange("p (k b) -> p k b", k=KF)[:, :, 0:B]

    def old_state(side, s):
        if s:
            return state[side][:, :, s - 1, :]
        return state[1 - side][:, :, CH - 1, :]

    @block.sync
    def _(sp):
        sp.dma_start(wih[:, :, :], io["wih"].rearrange("(k p) n -> p k n", p=P)).then_inc(w_in, 16)
        sp.dma_start(whh[:, :, :, :], io["whh"].rearrange("(k p) (j n) -> p k j n", p=P, j=KF)).then_inc(whh_in, 16)
        sp.dma_start(bias_i[:, :], io["b_ih"]).then_inc(w_in, 16)
        sp.dma_start(bias_h[:, :], io["b_hh"]).then_inc(w_in, 16)

        def chunk(c, side):
            sp.wait_ge(y_copied, c + 1)
            for s in range(CH):
                sp.dma_start(out_d[bass.ds(c * CH + s, 1), :, :].rearrange("o b f -> (o b) f"),
                             y_rows[B * s:B * s + B, :]).then_inc(y_out, 16)
        chunked(sp, chunk)
        sp.wait_ge(y_out, 16 * D)

    @block.gpsimd
    def _(pool):
        pool.memset(cond[:, :], 0.0).then_inc(zeroed, 1)
        pool.wait_ge(zeroed, 1)
        for k in range(KF):
            pool.dma_start(cond[DK * k:DK * k + B, :], io["mask"][:, P * k:P * k + P]).then_inc(cond_in, 16)

        def fetch(c, side):
            pool.tensor_copy(xc[side][:, :, :].rearrange("p k (t b) -> p k t b", t=CH),
                             xT[:, :, bass.ds(c * CH, CH), :]).then_inc(xc_made, 1)

        fetch(0, 0)

        def chunk(c, side):
            if not is_last(c):
                wait(pool, gi_made, GATES * c)
                wait(pool, y_made, c)
                fetch(c + 1, 1 - side)
            pool.wait_ge(state_made, c * CH + CH + 1)
            pool.wait_ge(xc_made, c + 1)
            wait(pool, y_done, c)
            pool.tensor_tensor(y[:, :, :], state[side][:, :, :, :].rearrange("p k s b -> p k (s b)"),
                               xc[side][:, :, :], ALU.add).then_inc(y_made, 1)
        chunked(pool, chunk)

    @block.scalar
    def _(act):
        def copy_y(c):
            act.wait_ge(y_done, c + 1)
            wait(act, y_out, 16 * CH * c)
            act.activation(y_rows[:, :], y_turned[:, :], ACT.Copy).then_inc(y_copied, 1)

        def chunk(c, side):
            for s in range(CH):
                t = c * CH + s
                act.wait_ge(rn_done, t + 1)
                act.activation(sum_rn[:, :], rn[:, 0:2 * P], ACT.Copy).then_inc(rn_copied, 1)
                act.wait_ge(rpre_made, t + 1)
                act.activation(r_gate[:, :, :], r_pre[:, :, :], ACT.Sigmoid).then_inc(r_made, 1)
                act.wait_ge(npre_made, t + 1)
                act.activation(n_gate[:, :, :], n_pre[:, :, :], ACT.Tanh).then_inc(n_made, 1)
                act.wait_ge(z_done, t + 1)
                act.activation(sum_z[:, :], z[:, 0:P], ACT.Copy).then_inc(z_copied, 1)
                act.wait_ge(zpre_made, t + 1)
                act.activation(z_gate[:, :, :], z_pre[:, :, :], ACT.Sigmoid).then_inc(z_made, 1)
                if s == 2 and not is_first(c):
                    copy_y(c - 1)
        act.wait_ge(psum_zeroed, 2)
        chunked(act, chunk)
        copy_y(CHUNKS - 1)

    @block.vector
    def _(dve):
        dve.memset(rn[:, :], 0.0).then_inc(psum_zeroed, 1)
        dve.memset(z[:, :], 0.0).then_inc(psum_zeroed, 1)
        dve.wait_ge(w_in, 48)
        dve.tensor_tensor(bias_i[:, 0:2 * KF], bias_i[:, 0:2 * KF], bias_h[:, 0:2 * KF],
                          ALU.add).then_inc(b_made, 1)
        dve.wait_ge(h0_turned, 1)
        dve.tensor_copy(state[1][:, :, CH - 1, :], turned(rn_turned, 0)).then_inc(state_made, 1)
        dve.wait_ge(b_made, 1)

        def bias(vec, q, shape):
            return vec[:, KF * q:KF * q + KF].rearrange("p (k o) -> p k o", o=1).to_broadcast(shape)

        def gates(c, side, q):
            dve.wait_ge(gi_summed, GATES * c + q + 1)
            dve.tensor_tensor(gi[side][:, q, :, :, :].rearrange("p k s b -> p k (s b)"),
                              gi_sum[q][:, :].rearrange("p (k n) -> p k n", k=KF),
                              bias(bias_i, q, [P, KF, CB]), ALU.add).then_inc(gi_made, 1)

        for q in range(GATES):
            gates(0, 0, q)

        def chunk(c, side):
            for s in range(CH):
                t = c * CH + s
                if s == 0:
                    dve.wait_ge(gi_made, GATES * c + GATES)
                    if not isinstance(c, int) or c >= 2:
                        dve.wait_ge(y_made, c - 1)
                dve.wait_ge(rnT_done, t + 1)
                dve.tensor_tensor(r_pre[:, :, :], turned(rn_turned, 0), gi[side][:, 0, :, s, :],
                                  ALU.add).then_inc(rpre_made, 1)
                dve.tensor_tensor(hn[:, :, :], turned(rn_turned, P), bias(bias_h, 2, [P, KF, B]),
                                  ALU.add).then_inc(hn_made, 1)
                dve.wait_ge(hn_made, t + 1)
                dve.wait_ge(r_made, t + 1)
                dve.tensor_tensor(rhn[:, :, :], r_gate[:, :, :], hn[:, :, :], ALU.mult).then_inc(rhn_made, 1)
                dve.wait_ge(rhn_made, t + 1)
                dve.tensor_tensor(n_pre[:, :, :], rhn[:, :, :], gi[side][:, 2, :, s, :],
                                  ALU.add).then_inc(npre_made, 1)
                dve.wait_ge(n_made, t + 1)
                dve.tensor_tensor(diff[:, :, :], old_state(side, s), n_gate[:, :, :],
                                  ALU.subtract).then_inc(diff_made, 1)
                dve.wait_ge(zT_done, t + 1)
                dve.tensor_tensor(z_pre[:, :, :], turned(z_turned, 0), gi[side][:, 1, :, s, :],
                                  ALU.add).then_inc(zpre_made, 1)
                dve.wait_ge(diff_made, t + 1)
                dve.wait_ge(z_made, t + 1)
                dve.tensor_tensor(zdiff[:, :, :], z_gate[:, :, :], diff[:, :, :], ALU.mult).then_inc(zdiff_made, 1)
                dve.wait_ge(zdiff_made, t + 1)
                dve.tensor_tensor(state[side][:, :, s, :], n_gate[:, :, :], zdiff[:, :, :],
                                  ALU.add).then_inc(state_made, 1)
                if s in EVAC and not is_last(c):
                    gates(c + 1, 1 - side, EVAC.index(s))
        chunked(dve, chunk)

    @block.tensor
    def _(pe):
        pe.wait_ge(cond_in, 16 * KF)
        pe.transpose(rn_turned[:, 0:P], cond[:, 0:P], ident[:, :]).then_inc(h0_turned, 1)
        pe.wait_ge(w_in, 48)
        pe.wait_ge(psum_zeroed, 2)

        def gate_sums(c, side, first, last):
            for f in range(first, min(last, GATES * KF * KF)):
                q, m, k = f // (KF * KF), f // KF % KF, f % KF
                if f == 0:
                    pe.wait_ge(xc_made, c + 1)
                if m == 0 and k == 0:
                    wait(pe, gi_made, GATES * (c - 1) + q + 1)
                at = T * q + P * m
                mm = pe.matmul(gi_sum[q][:, P * m:P * m + P], wih[:, k, at:at + P], xc[side][:, k, :],
                               start=(k == 0), stop=(k == KF - 1))
                if m == KF - 1 and k == KF - 1:
                    mm.then_inc(gi_summed, 1)

        def turn_y(c):
            pe.wait_ge(y_made, c + 1)
            wait(pe, y_copied, c)
            for k in range(KF):
                mm = pe.transpose(y_turned[:, P * k:P * k + P], y[:, k, :], ident[:, :])
            mm.then_inc(y_done, 1)

        gate_sums(0, 0, 0, GATES * KF * KF)
        pe.wait_ge(whh_in, 16)

        def recur(sums, side, s, k, first, last):
            for j in range(KF):
                mm = pe.matmul(sums[DK * j:DK * j + B, 0:last - first], old_state(side, s)[:, k, :],
                               whh[:, k, j, first:last], start=(k == 0), stop=(k == KF - 1))
            return mm

        def chunk(c, side):
            for s in range(CH):
                t = c * CH + s
                done = FILL * max(s - 1, 0)
                pe.wait_ge(state_made, t + 1)
                for k in range(KF):
                    mm = recur(rn, side, s, k, 0, 2 * P)
                mm.then_inc(rn_done, 1)
                for k in range(KF // 2):
                    recur(z, side, s, k, 2 * P, 3 * P)
                pe.wait_ge(rn_copied, t + 1)
                pe.transpose(rn_turned[:, 0:P], sum_rn[:, 0:P], ident[:, :])
                pe.transpose(rn_turned[:, P:2 * P], sum_rn[:, P:2 * P], ident[:, :]).then_inc(rnT_done, 1)
                for k in range(KF // 2, KF):
                    mm = recur(z, side, s, k, 2 * P, 3 * P)
                mm.then_inc(z_done, 1)
                if s and not is_last(c):
                    gate_sums(c + 1, 1 - side, done, done + 1)
                pe.wait_ge(z_copied, t + 1)
                pe.transpose(z_turned[:, 0:P], sum_z[:, :], ident[:, :]).then_inc(zT_done, 1)
                if s == 1 and not is_first(c):
                    turn_y(c - 1)
                if s and not is_last(c):
                    gate_sums(c + 1, 1 - side, done + 1, done + FILL)
        chunked(pe, chunk)
        turn_y(CHUNKS - 1)


def build(nc, io):
    with ExitStack() as ctx:
        xT = ctx.enter_context(nc.sbuf_tensor("xT", [P, KF, D, B], F32))
        ident = ctx.enter_context(nc.sbuf_tensor("ident", [P, P], F32))
        with ExitStack() as inner:
            attention(nc, inner, io, xT, ident)
        with ExitStack() as inner:
            gru(nc, inner, io, xT, ident)


def kernel(x, cond_2048, L0_cond_Wq, L0_cond_Wo, L1_cond_W_ih, L1_cond_W_hh, L1_cond_b_ih, L1_cond_b_hh):
    import numpy as np
    import concourse.bacc as bacc
    from concourse.bass_utils import run_bass_kernel_spmd

    w_hh = np.asarray(L1_cond_W_hh).reshape(T, GATES, KF, P)[:, [0, 2, 1]]
    arrays = {
        "x": x,
        "mask": cond_2048,
        "wq": np.asarray(L0_cond_Wq).T,
        "wo": np.asarray(L0_cond_Wo).T,
        "wih": L1_cond_W_ih,
        "whh": w_hh.transpose(0, 2, 1, 3).reshape(T, GATES * T),
        "b_ih": np.asarray(L1_cond_b_ih).reshape(GATES * KF, P).T,
        "b_hh": np.asarray(L1_cond_b_hh).reshape(GATES * KF, P).T,
        "ident": np.eye(P, dtype=np.float32),
        "diag": -np.kron(np.tile(np.eye(KT, dtype=np.float32), (HG, 1)), np.ones((1, P), np.float32)),
    }
    arrays = {name: np.ascontiguousarray(a) for name, a in arrays.items()}
    nc = bacc.Bacc("TRN2", target_bir_lowering=False, num_devices=1)
    io = {name: nc.dram_tensor("in_" + name, a.shape, F32, kind="ExternalInput").ap() for name, a in arrays.items()}
    io["out"] = nc.dram_tensor("out_0", (B, D, T), F32, kind="ExternalOutput").ap()
    io["live"] = nc.dram_tensor("live_rows", (B, T), BF16, kind="Internal").ap()
    io["dead"] = nc.dram_tensor("dead_rows", (B, T), BF16, kind="Internal").ap()
    build(nc, io)
    result = run_bass_kernel_spmd(nc, [{"in_" + name: a for name, a in arrays.items()}], core_ids=[0])
    return result.results[0]["out_0"]
```

```python
from contextlib import ExitStack

import concourse.bass as bass
from concourse import mybir

F32 = mybir.dt.float32
BF16 = mybir.dt.bfloat16
ALU = mybir.AluOpType
ACT = mybir.ActivationFunctionType
AX = mybir.AxisListType

P = 128
B = 16
D = 256
T = 512
NH = 8
DK = D // NH
HG = P // DK
NG = NH // HG
GROUPS = B * NG
KT = T // P
TILES = KT * HG
BIG = 1e30
SCALE = DK ** -0.5
PASS2 = 2 * DK + 2 * KT + 1
P_RING = 2

KF = T // P
CH = 8
CHUNKS = D // CH
CB = CH * B
FILL = 7
EVAC = [3, 5, 7]
GATES = 3


STACKED = 16 * (12 + 2)
PLACED = 16 * 2


def wait(eng, sem, value):
    if not isinstance(value, int) or value > 0:
        eng.wait_ge(sem, value)


def early(eng, value):
    return value if isinstance(value, int) else eng.compute_val(value)


def attention(nc, ctx, io, xT, ident, whh, wih, w_in):
    def sb(name, shape, dt=F32):
        return ctx.enter_context(nc.sbuf_tensor(name, shape, dt))

    def ps(name):
        return ctx.enter_context(nc.psum_tensor(name, [P, 512], F32))

    def sem(name):
        return ctx.enter_context(nc.semaphore(name))

    wq = sb("wq", [P, NG, D])
    wo = sb("wo", [P, NG, D])
    x_proj = sb("x_proj", [P, NG, T])
    x_res = sb("x_res", [P, NG, T])
    mask_cols = sb("mask_cols", [P, T])
    mask_rows = sb("mask_rows", [B, T])
    live = sb("live", [B, T], BF16)
    dead = sb("dead", [B, T], BF16)
    q_all = sb("q_all", [P, T])
    q_live = sb("q_live", [P, T])
    q_rest = sb("q_rest", [P, T])
    q_hi = sb("q_hi", [P, T], BF16)
    q_mid = sb("q_mid", [P, T], BF16)
    q_lo = sb("q_lo", [P, T], BF16)
    keys1 = [sb(f"keys1_{p}", [P, HG, T], BF16) for p in range(2)]
    qrys1 = [sb(f"qrys1_{p}", [P, HG, T], BF16) for p in range(2)]
    keys2 = [sb(f"keys2_{p}", [P, HG, T], BF16) for p in range(2)]
    qrys2 = [sb(f"qrys2_{p}", [P, HG, T], BF16) for p in range(2)]
    vals = [sb(f"vals_{p}", [P, KT, P]) for p in range(2)]
    probs = sb("probs", [P, P_RING, HG, T])
    row_max = sb("row_max", [P, HG * KT])
    diag = sb("diag", [HG * KT, KT, P])
    max_rows = sb("max_rows", [HG * KT, KT, P])
    max_hi = sb("max_hi", [HG * KT, KT, P], BF16)
    max_lo = sb("max_lo", [HG * KT, KT, P], BF16)
    ones = sb("ones", [P, DK])
    sums = sb("sums", [P, T])
    raw = sb("raw", [P, T])
    inv_sum = sb("inv_sum", [P, T])
    context = [sb(f"context_{g}", [P, T]) for g in range(NG)]

    peek = [ps(f"peek_{i}") for i in range(2)]
    score = [ps(f"score_{i}") for i in range(2)]
    pv = ps("pv")
    psum_p = ps("psum_p")
    small = ps("small")
    final = ps("final")

    const_in, x_in, mask_in, xres_in = sem("const_in"), sem("x_in"), sem("mask_in"), sem("xres_in")
    mrow_in, live_made, dead_made, mrow_out = sem("mrow_in"), sem("live_made"), sem("dead_made"), sem("mrow_out")
    ones_made = sem("ones_made")
    q_done, q_copied, q_masked = sem("q_done"), sem("q_copied"), sem("q_masked")
    hi_made, rest_made, mid_made, lo_made, rest2_made = (sem("hi_made"), sem("rest_made"), sem("mid_made"),
                                                         sem("lo_made"), sem("rest2_made"))
    stacked = sem("stacked")
    v_turned, v_copied = sem("v_turned"), sem("v_copied")
    peek_done, peek_used = sem("peek_done"), sem("peek_used")
    max_turned, max_spread, maxhi_made, maxlo_made, max_in = (sem("max_turned"), sem("max_spread"),
                                                              sem("maxhi_made"), sem("maxlo_made"), sem("max_in"))
    score_done, probs_made = sem("score_done"), sem("probs_made")
    round_done, inv_made, context_made = sem("round_done"), sem("inv_made"), sem("context_made")
    sums_copied = sem("sums_copied")
    final_done, final_used = sem("final_done"), sem("final_used")

    x_d = io["x"].rearrange("b (g p) t -> b p g t", p=P)

    def next_group(b, g, n=1):
        return (b, g + n) if g + n < NG else (b + (g + n) // NG, (g + n) % NG)

    def exists(b):
        return not isinstance(b, int) or 0 <= b < B

    def number(b, g):
        return b * NG + g

    block = ctx.enter_context(nc.Block())

    def staged(eng, stage):
        stage(-1, 0)
        stage(-1, 1)
        stage(0, 0)
        stage(0, 1)
        with eng.Fori(1, B - 1) as b:
            for g in range(NG):
                stage(b, g)
        stage(B - 1, 0)
        stage(B - 1, 1)
        stage(B, 0)

    @block.sync
    def _(sp):
        sp.dma_start(wq[:, :, :], io["wq"].rearrange("(g p) n -> p g n", p=P)).then_inc(const_in, 16)
        sp.dma_start(wo[:, :, :], io["wo"].rearrange("(g p) n -> p g n", p=P)).then_inc(const_in, 16)
        sp.dma_start(ident[:, :], io["ident"]).then_inc(const_in, 16)
        sp.dma_start(diag[:, :, :], io["diag"].rearrange("r (a c) -> r a c", a=KT)).then_inc(const_in, 16)

        def load_x(b):
            wait(sp, q_done, number(b, 0))
            sp.dma_start(x_proj[:, :, :], x_d[b]).then_inc(x_in, 16)
            wait(sp, q_masked, number(b, 0))
            sp.dma_start(mask_cols[:, :], io["mask"][bass.ds(b, 1), :].partition_broadcast(P)).then_inc(mask_in, 16)

        def stack(b, g):
            n = number(b, g)
            made_at, read_at = early(sp, n + 1), early(sp, TILES * (n - 1))
            wait(sp, score_done, read_at)
            for part, made, places in (
                (q_hi, hi_made, ((keys1, 0), (qrys1, 0), (qrys1, 1), (keys1, 2), (qrys1, 3), (keys2, 0))),
                (q_mid, mid_made, ((keys1, 1), (qrys1, 2), (keys2, 1), (qrys2, 1))),
                (q_lo, lo_made, ((keys1, 3), (qrys2, 0))),
            ):
                sp.wait_ge(made, made_at)
                for buffers, quarter in places:
                    sp.dma_start(buffers[g][DK * quarter:DK * quarter + DK, :, :],
                                 part[:, :]).then_inc(stacked, 16)
            at = 2 * DK + 2 * KT
            for buffers, row in ((keys2, "dead"), (qrys2, "live")):
                sp.dma_start(buffers[g][at:at + 1, :, :],
                             io[row][bass.ds(b, 1), :].rearrange("o (h t) -> o h t", h=1)
                             .to_broadcast([1, HG, T])).then_inc(stacked, 16)

        def place_max(b, g):
            n = number(b, g)
            for part, made, at in ((max_hi, maxhi_made, 2 * DK), (max_lo, maxlo_made, 2 * DK + KT)):
                sp.wait_ge(made, n + 1)
                sp.dma_start(qrys2[g][at:at + KT, :, :], part[:, :, :]).then_inc(max_in, 16)

        def stage(b, g):
            b1, g1 = next_group(b, g)
            b2, g2 = next_group(b, g, 2)
            if isinstance(b, int) and (b, g) == (0, 1):
                sp.dma_start(wih[:, :, :], io["wih"].rearrange("(k p) n -> p k n", p=P)).then_inc(w_in, 16)
                sp.dma_start(whh[:, :, :, :],
                             io["whh"].rearrange("(k p) (j n) -> p k j n", p=P, j=KF)).then_inc(w_in, 16)
            if exists(b1):
                stack(b1, g1)
            if g2 == 0 and exists(b2):
                load_x(b2)
            if g == NG - 1 and exists(b):
                wait(sp, final_done, 2 * b)
                sp.dma_start(x_res[:, :, :], x_d[b]).then_inc(xres_in, 16)
            if exists(b1):
                place_max(b1, g1)

        sp.wait_ge(mrow_out, 32)
        sp.wait_ge(ones_made, 5)
        staged(sp, stage)

    @block.gpsimd
    def _(pool):
        for buf in (*keys2, *qrys2):
            pool.memset(buf[2 * DK:PASS2 + 23, :, :], 1.0).then_inc(ones_made, 1)
        pool.wait_ge(ones_made, len(keys2) + len(qrys2))
        pool.memset(ones[:, :], 1.0).then_inc(ones_made, 1)
        pool.dma_start(mask_rows[:, :], io["mask"]).then_inc(mrow_in, 16)
        pool.wait_ge(live_made, 1)
        pool.dma_start(io["live"], live[:, :]).then_inc(mrow_out, 16)
        pool.wait_ge(dead_made, 2)
        pool.dma_start(io["dead"], dead[:, :]).then_inc(mrow_out, 16)

        def stage(b, g):
            b2, g2 = next_group(b, g, 2)
            if not exists(b2):
                return
            n = number(b2, g2)
            pool.wait_ge(mid_made, n + 1)
            wait(pool, stacked, STACKED * n)
            pool.tensor_tensor(q_lo[:, :], q_rest[:, :], q_mid[:, :], ALU.subtract).then_inc(lo_made, 1)

        staged(pool, stage)

    @block.scalar
    def _(act):
        def project(b, g):
            n = number(b, g)
            act.wait_ge(q_masked, n + 1)
            wait(act, v_turned, n)
            act.activation(q_all[:, :], small[:, :], ACT.Copy).then_inc(q_copied, 1)
            wait(act, stacked, STACKED * n)
            act.activation(q_hi[:, :], q_live[:, :], ACT.Copy).then_inc(hi_made, 1)
            act.wait_ge(rest_made, n + 1)
            act.activation(q_mid[:, :], q_rest[:, :], ACT.Copy).then_inc(mid_made, 1)

        def values(b, g):
            n = number(b, g)
            act.wait_ge(v_turned, n + 1)
            wait(act, round_done, KT * (n - 1))
            act.activation(vals[g][:, :, :].rearrange("p a c -> p (a c)"), small[:, :],
                           ACT.Copy).then_inc(v_copied, 1)

        def finish(b):
            for half in range(2):
                act.wait_ge(final_done, 2 * b + half + 1)
                act.activation(xT[:, 2 * half:2 * half + 2, :, bass.ds(b, 1)].rearrange("p k t o -> p k (t o)"),
                               final[:, :].rearrange("p (k t) -> p k t", k=2), ACT.Copy).then_inc(final_used, 1)

        def stage(b, g):
            b1, g1 = next_group(b, g)
            b2, g2 = next_group(b, g, 2)
            n = number(b, g)
            for i in range(KT):
                if exists(b):
                    for h in range(HG):
                        act.wait_ge(score_done, TILES * n + HG * i + h + 1)
                        if h == 0 and (not isinstance(b, int) or KT * n + i >= P_RING):
                            act.wait_ge(round_done, KT * n + i - P_RING + 1)
                        act.activation(probs[:, i % P_RING, h, :], score[h % 2][:, :], ACT.Exp,
                                       scale=SCALE).then_inc(probs_made, 1)
                if i == 1 and exists(b1):
                    values(b1, g1)
                if i == 2 and g == 0 and exists(b - 1):
                    finish(b - 1)
            if exists(b2):
                project(b2, g2)

        staged(act, stage)

    @block.vector
    def _(dve):
        dve.wait_ge(mrow_in, 16)
        dve.tensor_copy(live[:, :], mask_rows[:, :]).then_inc(live_made, 1)
        dve.tensor_scalar(mask_rows[:, :], mask_rows[:, :], -1.0, None, ALU.add).then_inc(dead_made, 1)
        dve.wait_ge(dead_made, 1)
        dve.tensor_scalar(dead[:, :], mask_rows[:, :], BIG, None, ALU.mult).then_inc(dead_made, 1)

        def project(b, g):
            n = number(b, g)
            dve.wait_ge(q_done, n + 1)
            dve.wait_ge(mask_in, 16 * (b + 1))
            wait(dve, hi_made, n)
            dve.tensor_tensor(q_live[:, :], small[:, :], mask_cols[:, :], ALU.mult).then_inc(q_masked, 1)
            dve.wait_ge(hi_made, n + 1)
            dve.wait_ge(q_masked, n + 1)
            wait(dve, lo_made, n)
            dve.tensor_tensor(q_rest[:, :], q_live[:, :], q_hi[:, :], ALU.subtract).then_inc(rest_made, 1)

        def maxima(b, g):
            n = number(b, g)
            wait(dve, max_turned, n)
            for i in range(KT):
                for h in range(HG):
                    dve.wait_ge(peek_done, TILES * n + HG * i + h + 1)
                    dve.tensor_reduce(row_max[:, HG * i + h:HG * i + h + 1], peek[h % 2][:, :], AX.X,
                                      ALU.max).then_inc(peek_used, 1)

        def spread(b, g):
            n = number(b, g)
            dve.wait_ge(max_turned, n + 1)
            turned = small[0:HG * KT, 0:P].rearrange("r (o c) -> r o c", o=1).to_broadcast([HG * KT, KT, P])
            dve.tensor_tensor(max_rows[:, :, :], turned, diag[:, :, :], ALU.mult).then_inc(max_spread, 1)
            dve.wait_ge(max_spread, n + 1)
            wait(dve, max_in, PLACED * n)
            dve.tensor_copy(max_hi[:, :, :], max_rows[:, :, :]).then_inc(maxhi_made, 1)
            dve.wait_ge(maxhi_made, n + 1)
            dve.tensor_tensor(max_lo[:, :, :], max_rows[:, :, :], max_hi[:, :, :],
                              ALU.subtract).then_inc(maxlo_made, 1)

        def normalise(b, g):
            n = number(b, g)
            dve.wait_ge(round_done, KT * (n + 1))
            dve.tensor_copy(sums[:, :], psum_p[:, :]).then_inc(sums_copied, 1)
            wait(dve, context_made, n)
            dve.tensor_copy(raw[:, :], pv[:, :]).then_inc(sums_copied, 1)
            dve.wait_ge(sums_copied, 2 * n + 2)
            dve.reciprocal(inv_sum[:, :], sums[:, :]).then_inc(inv_made, 1)
            dve.wait_ge(inv_made, n + 1)
            if not isinstance(b, int) or b >= 1:
                dve.wait_ge(final_done, 2 * b)
            dve.tensor_tensor(context[g][:, :], raw[:, :], inv_sum[:, :], ALU.mult).then_inc(context_made, 1)

        def stage(b, g):
            b0, g0 = (b, g - 1) if g else (b - 1, NG - 1)
            b1, g1 = next_group(b, g)
            b2, g2 = next_group(b, g, 2)
            if exists(b0):
                normalise(b0, g0)
            if exists(b1):
                maxima(b1, g1)
                spread(b1, g1)
            if exists(b2):
                project(b2, g2)

        dve.wait_ge(const_in, 64)
        staged(dve, stage)

    @block.tensor
    def _(pe):
        pe.wait_ge(const_in, 64)
        pe.wait_ge(ones_made, 5)

        def project(b, g):
            n = number(b, g)
            pe.wait_ge(x_in, 16 * (b + 1))
            wait(pe, max_spread, n)
            for k in range(NG):
                mm = pe.matmul(small[:, :], wq[:, k, P * g:P * g + P], x_proj[:, k, :],
                               start=(k == 0), stop=(k == NG - 1))
            mm.then_inc(q_done, 1)

        def peeks(b, g, i):
            n = number(b, g)
            if i == 0:
                pe.wait_ge(stacked, STACKED * (n + 1))
            for h in range(HG):
                wait(pe, peek_used, TILES * n + HG * i + h - 1)
                pe.matmul(peek[h % 2][:, :], keys1[g][:, h, P * i:P * i + P], qrys1[g][:, h, :],
                          start=True, stop=True).then_inc(peek_done, 1)

        def turn_max(b, g):
            n = number(b, g)
            pe.wait_ge(peek_used, TILES * (n + 1))
            pe.wait_ge(v_copied, n + 1)
            pe.transpose(small[0:HG * KT, 0:P], row_max[:, :], ident[:, :]).then_inc(max_turned, 1)

        def turn_values(b, g):
            n = number(b, g)
            pe.wait_ge(q_copied, n + 1)
            for a in range(KT):
                mm = pe.transpose(small[:, P * a:P * a + P], q_all[:, P * a:P * a + P], ident[:, :])
            mm.then_inc(v_turned, 1)

        def scores(b, g, i):
            n = number(b, g)
            for h in range(HG):
                wait(pe, probs_made, TILES * n + HG * i + h - 1)
                pe.matmul(score[h % 2][:, :], keys1[g][:, h, P * i:P * i + P], qrys1[g][:, h, :],
                          start=True, stop=False)
                if i == 0 and h == 0:
                    pe.wait_ge(max_in, PLACED * (n + 1))
                pe.matmul(score[h % 2][:, :], keys2[g][0:PASS2, h, P * i:P * i + P], qrys2[g][0:PASS2, h, :],
                          start=False, stop=True).then_inc(score_done, 1)

        def weigh(b, g, i):
            n = number(b, g)
            if i == 0:
                wait(pe, sums_copied, 2 * n)
                pe.wait_ge(v_copied, n + 1)
            pe.wait_ge(probs_made, TILES * n + HG * (i + 1))
            for h in range(HG):
                pe.matmul(pv[DK * h:DK * h + DK, :], vals[g][:, i, h:P:HG], probs[:, i % P_RING, h, :],
                          start=(i == 0), stop=(i == KT - 1))
            for h in range(HG):
                mm = pe.matmul(psum_p[DK * h:DK * h + DK, :], ones[:, :], probs[:, i % P_RING, h, :],
                               start=(i == 0), stop=(i == KT - 1))
            mm.then_inc(round_done, 1)

        def finish(b):
            pe.wait_ge(context_made, NG * (b + 1))
            pe.wait_ge(xres_in, 16 * (b + 1))
            for half in range(2):
                wait(pe, final_used, 2 * b + half)
                for kk in range(2):
                    k = 2 * half + kk
                    at = D * kk
                    for g in range(NG):
                        pe.matmul(final[:, at + P * g:at + P * g + P], x_res[:, g, P * k:P * k + P], ident[:, :],
                                  start=(kk == 0 and g == 0), stop=False, is_transpose=True, skip_group_check=True)
                    for g in range(NG):
                        mm = pe.matmul(final[:, at:at + D], context[g][:, P * k:P * k + P], wo[:, g, :],
                                       start=False, stop=(g == NG - 1), skip_group_check=True)
                mm.then_inc(final_done, 1)

        def stage(b, g):
            b0, g0 = (b, g - 1) if g else (b - 1, NG - 1)
            b1, g1 = next_group(b, g)
            b2, g2 = next_group(b, g, 2)
            for i in range(KT):
                if exists(b):
                    scores(b, g, i)
                if i == 0 and exists(b0):
                    weigh(b0, g0, KT - 1)
                if i >= 1 and exists(b):
                    weigh(b, g, i - 1)
                if exists(b1):
                    peeks(b1, g1, i)
                if i == 0 and exists(b1):
                    turn_values(b1, g1)
                if i == 2 and g == 0 and exists(b0):
                    finish(b0)
            if exists(b1):
                turn_max(b1, g1)
            if exists(b2):
                project(b2, g2)

        staged(pe, stage)


def gru(nc, ctx, io, xT, ident, whh, wih, w_in):
    def sb(name, shape, dt=F32):
        return ctx.enter_context(nc.sbuf_tensor(name, shape, dt))

    def ps(name):
        return ctx.enter_context(nc.psum_tensor(name, [P, 512], F32))

    def sem(name):
        return ctx.enter_context(nc.semaphore(name))

    bias_i = sb("bias_i", [P, GATES * KF])
    bias_h = sb("bias_h", [P, GATES * KF])
    state = [sb(f"state_{c}", [P, KF, CH, B]) for c in range(2)]
    cond = sb("cond", [P, P])
    xc = [sb(f"xc_{c}", [P, KF, CB]) for c in range(2)]
    gi = [sb(f"gi_{c}", [P, GATES, KF, CH, B]) for c in range(2)]
    sum_r, sum_n, sum_z = sb("sum_r", [P, P]), sb("sum_n", [P, P]), sb("sum_z", [P, P])
    cond_turned = sb("cond_turned", [P, P])
    r_pre, r_gate, hn, rhn, n_pre, n_gate, z_pre, z_gate, diff, zdiff = (
        sb(name, [P, KF, B]) for name in ("r_pre", "r_gate", "hn", "rhn", "n_pre", "n_gate",
                                          "z_pre", "z_gate", "diff", "zdiff"))
    y = sb("y", [P, KF, CB])
    y_rows = sb("y_rows", [P, T])

    rn = ps("rn")
    z = ps("z")
    gi_sum = [ps(f"gi_sum_{q}") for q in range(GATES)]
    y_turned = ps("y_turned")

    b_in, cond_in, b_made, zeroed, psum_zeroed = (sem("b_in"), sem("cond_in"), sem("b_made"), sem("zeroed"),
                                                  sem("psum_zeroed"))
    h0_turned, state_made = sem("h0_turned"), sem("state_made")
    xc_made, gi_summed, gi_made = sem("xc_made"), sem("gi_summed"), sem("gi_made")
    rn_done, z_done, r_turned, n_turned, z_turned = (
        sem("rn_done"), sem("z_done"), sem("r_turned"), sem("n_turned"), sem("z_turned"))
    rpre_made, hn_made, r_made, rhn_made, npre_made, n_made = (
        sem("rpre_made"), sem("hn_made"), sem("r_made"), sem("rhn_made"), sem("npre_made"), sem("n_made"))
    zpre_made, z_made, diff_made, zdiff_made = sem("zpre_made"), sem("z_made"), sem("diff_made"), sem("zdiff_made")
    y_made, y_done, y_copied, y_out = sem("y_made"), sem("y_done"), sem("y_copied"), sem("y_out")

    out_d = io["out"].rearrange("b t f -> t b f")

    block = ctx.enter_context(nc.Block())

    def chunked(eng, chunk):
        chunk(0, 0)
        chunk(1, 1)
        with eng.Fori(1, CHUNKS // 2 - 1) as pair:
            chunk(2 * pair, 0)
            chunk(2 * pair + 1, 1)
        chunk(CHUNKS - 2, 0)
        chunk(CHUNKS - 1, 1)

    def is_first(c):
        return isinstance(c, int) and c == 0

    def is_last(c):
        return isinstance(c, int) and c == CHUNKS - 1

    def batches(sums):
        return sums[:, :].rearrange("p (k b) -> p k b", k=KF)[:, :, 0:B]

    def old_state(side, s):
        if s:
            return state[side][:, :, s - 1, :]
        return state[1 - side][:, :, CH - 1, :]

    @block.sync
    def _(sp):
        sp.dma_start(bias_i[:, :], io["b_ih"]).then_inc(b_in, 16)
        sp.dma_start(bias_h[:, :], io["b_hh"]).then_inc(b_in, 16)

        def chunk(c, side):
            sp.wait_ge(y_copied, c + 1)
            sp.dma_start(out_d[bass.ds(c * CH, CH), :, :], y_rows[:, :]).then_inc(y_out, 16)
        chunked(sp, chunk)
        sp.wait_ge(y_out, 16 * CHUNKS)

    @block.gpsimd
    def _(pool):
        pool.memset(cond[:, :], 0.0).then_inc(zeroed, 1)
        pool.wait_ge(zeroed, 1)
        for k in range(KF):
            pool.dma_start(cond[DK * k:DK * k + B, :],
                           io["mask"].rearrange("b (k j u) -> b k j u", k=KF, j=KF)[:, :, k, :]).then_inc(cond_in, 16)

        def fetch(c, side):
            pool.tensor_copy(xc[side][:, :, :].rearrange("p k (t b) -> p k t b", t=CH),
                             xT[:, :, bass.ds(c * CH, CH), :]).then_inc(xc_made, 1)

        fetch(0, 0)

        def chunk(c, side):
            if not is_last(c):
                wait(pool, gi_made, GATES * c)
                wait(pool, y_made, c)
                fetch(c + 1, 1 - side)
            pool.wait_ge(state_made, c * CH + CH + 1)
            pool.wait_ge(xc_made, c + 1)
            wait(pool, y_done, c)
            pool.tensor_tensor(y[:, :, :], state[side][:, :, :, :].rearrange("p k s b -> p k (s b)"),
                               xc[side][:, :, :], ALU.add).then_inc(y_made, 1)
        chunked(pool, chunk)

    @block.scalar
    def _(act):
        def copy_y(c):
            act.wait_ge(y_done, c + 1)
            wait(act, y_out, 16 * c)
            act.activation(y_rows[:, :], y_turned[:, :], ACT.Copy).then_inc(y_copied, 1)

        def chunk(c, side):
            for s in range(CH):
                t = c * CH + s
                act.wait_ge(rpre_made, t + 1)
                act.activation(r_gate[:, :, :], r_pre[:, :, :], ACT.Sigmoid).then_inc(r_made, 1)
                act.wait_ge(npre_made, t + 1)
                act.activation(n_gate[:, :, :], n_pre[:, :, :], ACT.Tanh).then_inc(n_made, 1)
                act.wait_ge(zpre_made, t + 1)
                act.activation(z_gate[:, :, :], z_pre[:, :, :], ACT.Sigmoid).then_inc(z_made, 1)
                if s == 2 and not is_first(c):
                    copy_y(c - 1)
        chunked(act, chunk)
        copy_y(CHUNKS - 1)

    @block.vector
    def _(dve):
        dve.memset(rn[:, :], 0.0).then_inc(psum_zeroed, 1)
        dve.memset(z[:, :], 0.0).then_inc(psum_zeroed, 1)
        dve.wait_ge(b_in, 32)
        dve.tensor_tensor(bias_i[:, 0:2 * KF], bias_i[:, 0:2 * KF], bias_h[:, 0:2 * KF],
                          ALU.add).then_inc(b_made, 1)
        dve.wait_ge(cond_in, 16 * KF)
        dve.transpose(cond_turned[:, :], cond[:, :]).then_inc(h0_turned, 1)
        dve.wait_ge(h0_turned, 1)
        dve.tensor_copy(state[1][:, :, CH - 1, :], batches(cond_turned)).then_inc(state_made, 1)
        dve.wait_ge(b_made, 1)

        def bias(vec, q, shape):
            return vec[:, KF * q:KF * q + KF].rearrange("p (k o) -> p k o", o=1).to_broadcast(shape)

        def gates(c, side, q):
            dve.wait_ge(gi_summed, GATES * c + q + 1)
            dve.tensor_tensor(gi[side][:, q, :, :, :].rearrange("p k s b -> p k (s b)"),
                              gi_sum[q][:, :].rearrange("p (k n) -> p k n", k=KF),
                              bias(bias_i, q, [P, KF, CB]), ALU.add).then_inc(gi_made, 1)

        for q in range(GATES):
            gates(0, 0, q)

        def chunk(c, side):
            for s in range(CH):
                t = c * CH + s
                if s == 0:
                    dve.wait_ge(gi_made, GATES * c + GATES)
                    if not isinstance(c, int) or c >= 2:
                        dve.wait_ge(y_made, c - 1)
                dve.wait_ge(rn_done, t + 1)
                dve.transpose(sum_r[:, :], rn[:, 0:P]).then_inc(r_turned, 1)
                dve.wait_ge(r_turned, t + 1)
                dve.tensor_tensor(r_pre[:, :, :], batches(sum_r), gi[side][:, 0, :, s, :],
                                  ALU.add).then_inc(rpre_made, 1)
                dve.transpose(sum_n[:, :], rn[:, P:2 * P]).then_inc(n_turned, 1)
                dve.wait_ge(n_turned, t + 1)
                dve.tensor_tensor(hn[:, :, :], batches(sum_n), bias(bias_h, 2, [P, KF, B]),
                                  ALU.add).then_inc(hn_made, 1)
                dve.wait_ge(hn_made, t + 1)
                dve.wait_ge(r_made, t + 1)
                dve.tensor_tensor(rhn[:, :, :], r_gate[:, :, :], hn[:, :, :], ALU.mult).then_inc(rhn_made, 1)
                dve.wait_ge(rhn_made, t + 1)
                dve.tensor_tensor(n_pre[:, :, :], rhn[:, :, :], gi[side][:, 2, :, s, :],
                                  ALU.add).then_inc(npre_made, 1)
                dve.wait_ge(z_done, t + 1)
                dve.transpose(sum_z[:, :], z[:, 0:P]).then_inc(z_turned, 1)
                dve.wait_ge(z_turned, t + 1)
                dve.tensor_tensor(z_pre[:, :, :], batches(sum_z), gi[side][:, 1, :, s, :],
                                  ALU.add).then_inc(zpre_made, 1)
                dve.wait_ge(n_made, t + 1)
                dve.tensor_tensor(diff[:, :, :], old_state(side, s), n_gate[:, :, :],
                                  ALU.subtract).then_inc(diff_made, 1)
                dve.wait_ge(diff_made, t + 1)
                dve.wait_ge(z_made, t + 1)
                dve.tensor_tensor(zdiff[:, :, :], z_gate[:, :, :], diff[:, :, :], ALU.mult).then_inc(zdiff_made, 1)
                dve.wait_ge(zdiff_made, t + 1)
                dve.tensor_tensor(state[side][:, :, s, :], n_gate[:, :, :], zdiff[:, :, :],
                                  ALU.add).then_inc(state_made, 1)
                if s in EVAC and not is_last(c):
                    gates(c + 1, 1 - side, EVAC.index(s))
        chunked(dve, chunk)

    @block.tensor
    def _(pe):
        pe.wait_ge(w_in, 32)
        pe.wait_ge(psum_zeroed, 2)

        def gate_sums(c, side, first, last):
            for f in range(first, min(last, GATES * KF * KF)):
                q, m, k = f // (KF * KF), f // KF % KF, f % KF
                if f == 0:
                    pe.wait_ge(xc_made, c + 1)
                if m == 0 and k == 0:
                    wait(pe, gi_made, GATES * (c - 1) + q + 1)
                at = T * q + P * m
                mm = pe.matmul(gi_sum[q][:, P * m:P * m + P], wih[:, k, at:at + P], xc[side][:, k, :],
                               start=(k == 0), stop=(k == KF - 1))
                if m == KF - 1 and k == KF - 1:
                    mm.then_inc(gi_summed, 1)

        def turn_y(c):
            pe.wait_ge(y_made, c + 1)
            wait(pe, y_copied, c)
            for k in range(KF):
                mm = pe.transpose(y_turned[:, P * k:P * k + P], y[:, k, :], ident[:, :])
            mm.then_inc(y_done, 1)

        gate_sums(0, 0, 0, GATES * KF * KF)
        def recur(sums, side, s, k, first, last):
            for j in range(KF):
                mm = pe.matmul(sums[DK * j:DK * j + B, 0:last - first], old_state(side, s)[:, k, :],
                               whh[:, k, j, first:last], start=(k == 0), stop=(k == KF - 1))
            return mm

        def chunk(c, side):
            for s in range(CH):
                t = c * CH + s
                done = FILL * max(s - 1, 0)
                pe.wait_ge(state_made, t + 1)
                for k in range(KF):
                    mm = recur(rn, side, s, k, 0, 2 * P)
                mm.then_inc(rn_done, 1)
                for k in range(KF):
                    mm = recur(z, side, s, k, 2 * P, 3 * P)
                mm.then_inc(z_done, 1)
                if s == 1 and not is_first(c):
                    turn_y(c - 1)
                if s and not is_last(c):
                    gate_sums(c + 1, 1 - side, done, done + FILL)
        chunked(pe, chunk)
        turn_y(CHUNKS - 1)


def build(nc, io):
    with ExitStack() as ctx:
        xT = ctx.enter_context(nc.sbuf_tensor("xT", [P, KF, D, B], F32))
        ident = ctx.enter_context(nc.sbuf_tensor("ident", [P, P], F32))
        whh = ctx.enter_context(nc.sbuf_tensor("whh", [P, KF, KF, GATES * P], F32))
        wih = ctx.enter_context(nc.sbuf_tensor("wih", [P, KF, GATES * T], F32))
        w_in = ctx.enter_context(nc.semaphore("w_in"))
        with ExitStack() as inner:
            attention(nc, inner, io, xT, ident, whh, wih, w_in)
        with ExitStack() as inner:
            gru(nc, inner, io, xT, ident, whh, wih, w_in)


def kernel(x, cond_2048, L0_cond_Wq, L0_cond_Wo, L1_cond_W_ih, L1_cond_W_hh, L1_cond_b_ih, L1_cond_b_hh):
    import numpy as np
    import concourse.bacc as bacc
    from concourse.bass_utils import run_bass_kernel_spmd

    w_hh = np.asarray(L1_cond_W_hh).reshape(T, GATES, KF, KF, DK)[:, [0, 2, 1]]
    arrays = {
        "x": x,
        "mask": cond_2048,
        "wq": np.asarray(L0_cond_Wq).T.reshape(D, NG, HG, DK).transpose(0, 1, 3, 2).reshape(D, D),
        "wo": np.asarray(L0_cond_Wo).T,
        "wih": L1_cond_W_ih,
        "whh": w_hh.transpose(0, 3, 1, 2, 4).reshape(T, GATES * T),
        "b_ih": np.asarray(L1_cond_b_ih).reshape(GATES * KF, P).T,
        "b_hh": np.asarray(L1_cond_b_hh).reshape(GATES * KF, P).T,
        "ident": np.eye(P, dtype=np.float32),
        "diag": -np.kron(np.eye(KT, dtype=np.float32), np.ones((HG, P), np.float32)),
    }
    arrays = {name: np.ascontiguousarray(a) for name, a in arrays.items()}
    nc = bacc.Bacc("TRN2", target_bir_lowering=False, num_devices=1)
    io = {name: nc.dram_tensor("in_" + name, a.shape, F32, kind="ExternalInput").ap() for name, a in arrays.items()}
    io["out"] = nc.dram_tensor("out_0", (B, D, T), F32, kind="ExternalOutput").ap()
    io["live"] = nc.dram_tensor("live_rows", (B, T), BF16, kind="Internal").ap()
    io["dead"] = nc.dram_tensor("dead_rows", (B, T), BF16, kind="Internal").ap()
    build(nc, io)
    result = run_bass_kernel_spmd(nc, [{"in_" + name: a for name, a in arrays.items()}], core_ids=[0])
    return result.results[0]["out_0"]
```

```python
from contextlib import ExitStack

import concourse.bass as bass
from concourse import mybir

F32 = mybir.dt.float32
BF16 = mybir.dt.bfloat16
ALU = mybir.AluOpType
ACT = mybir.ActivationFunctionType
AX = mybir.AxisListType

P = 128
B = 16
D = 256
T = 512
NH = 8
DK = D // NH
HG = P // DK
NG = NH // HG
GROUPS = B * NG
KT = T // P
TILES = KT * HG
BIG = 1e30
SCALE = DK ** -0.5
MAX_AT, MASK_AT = 2 * DK, 2 * DK + 2
PASS2 = MASK_AT + 1
RING = 6
PEEKS = [0, 0, 1, 3, 5, 5, 7, 8, 10, 12, 13, 15, 16, 16, 16, 16, 16]
P_RING = 3
ADDS = (KT - 1) * HG
READ_BY = [HG, *(HG * i for i in range(1, KT))]

KF = T // P
CH = 8
CHUNKS = D // CH
CB = CH * B
GATES = 3
FILL = GATES * KF * KF // CH
EVAC = [2, 5, 7]


STACKED = 16 * (12 + 2)
PLACED = 16 * 2


def wait(eng, sem, value):
    if not isinstance(value, int) or value > 0:
        eng.wait_ge(sem, value)


class Group:

    def __init__(self, turn, c):
        self.turn, self.c = turn, c
        self.n = c if isinstance(turn, int) else turn * RING + c
        self.batch = c // NG if isinstance(turn, int) else turn * (RING // NG) + c // NG
        self.half, self.third = c % NG, c % 3

    @property
    def exists(self):
        return not isinstance(self.n, int) or 0 <= self.n < GROUPS

    def shift(self, k):
        return Group(self.turn, self.c + k)

    def is_at(self, n):
        return isinstance(self.n, int) and self.n == n


def early(eng, value):
    return value if isinstance(value, int) else eng.compute_val(value)


def attention(nc, ctx, io, xT, ident, wih, w_in):
    def sb(name, shape, dt=F32):
        return ctx.enter_context(nc.sbuf_tensor(name, shape, dt))

    def ps(name):
        return ctx.enter_context(nc.psum_tensor(name, [P, 512], F32))

    def sem(name):
        return ctx.enter_context(nc.semaphore(name))

    wq = sb("wq", [P, NG, D])
    wo = sb("wo", [P, NG, D])
    x_proj = sb("x_proj", [P, NG, T])
    x_res = sb("x_res", [P, NG, T])
    mask_cols = sb("mask_cols", [P, T])
    q_all = sb("q_all", [P, T])
    q_live = sb("q_live", [P, T])
    q_hi = sb("q_hi", [P, T], BF16)
    q_mid = sb("q_mid", [P, T], BF16)
    q_lo = sb("q_lo", [P, T], BF16)
    keys1 = [sb(f"keys1_{p}", [P, HG, T], BF16) for p in range(3)]
    qrys1 = [sb(f"qrys1_{p}", [P, HG, T], BF16) for p in range(3)]
    keys2 = [sb(f"keys2_{p}", [P, HG, T], BF16) for p in range(3)]
    qrys2 = [sb(f"qrys2_{p}", [P, HG, T], BF16) for p in range(3)]
    vals = [sb(f"vals_{p}", [P, KT, P]) for p in range(3)]
    probs = sb("probs", [P, P_RING, HG, T])
    total = sb("total", [P, HG, T])
    row_max = sb("row_max", [P, HG * KT])
    max_hi = sb("max_hi", [HG * KT, P], BF16)
    max_lo = sb("max_lo", [HG * KT, P], BF16)
    ones = sb("ones", [P, DK])
    raw = sb("raw", [P, T])
    inv_sum = sb("inv_sum", [P, T])
    live = sb("live", [B, T], BF16)
    dead = sb("dead", [B, T], BF16)
    mask_rows = raw[0:B, :]
    context = [sb(f"context_{g}", [P, T]) for g in range(NG)]

    peek = [ps(f"peek_{i}") for i in range(2)]
    score = [ps(f"score_{i}") for i in range(2)]
    pv = ps("pv")
    psum_p = ps("psum_p")
    small = ps("small")
    final = ps("final")

    const_in, x_in, mask_in, xres_in = sem("const_in"), sem("x_in"), sem("mask_in"), sem("xres_in")
    mrow_in, live_made, dead_made, mrow_out = sem("mrow_in"), sem("live_made"), sem("dead_made"), sem("mrow_out")
    ones_made = sem("ones_made")
    q_done, q_copied, q_masked = sem("q_done"), sem("q_copied"), sem("q_masked")
    hi_made, rest_made, mid_made, lo_made, rest2_made = (sem("hi_made"), sem("rest_made"), sem("mid_made"),
                                                         sem("lo_made"), sem("rest2_made"))
    stacked = sem("stacked")
    v_turned, v_copied = sem("v_turned"), sem("v_copied")
    peek_done, peek_used = sem("peek_done"), sem("peek_used")
    max_turned, maxhi_made, maxlo_made, max_in = (sem("max_turned"), sem("maxhi_made"), sem("maxlo_made"),
                                                  sem("max_in"))
    score_done, probs_made = sem("score_done"), sem("probs_made")
    round_done, inv_made, context_made = sem("round_done"), sem("inv_made"), sem("context_made")
    added, total_done, raw_copied = sem("added"), sem("total_done"), sem("raw_copied")
    final_done, final_used = sem("final_done"), sem("final_used")

    x_d = io["x"].rearrange("b (g p) t -> b p g t", p=P)

    block = ctx.enter_context(nc.Block())

    def staged(eng, stage):
        for c in range(-2, RING):
            stage(Group(0, c))
        with eng.Fori(1, GROUPS // RING) as turn:
            for c in range(RING):
                stage(Group(turn, c))
        for c in range(GROUPS // RING * RING, GROUPS + 2):
            stage(Group(0, c))

    def finished(G):
        return G.shift(-NG) if G.half == NG - 1 else None

    def place(G, i):
        return (KT * G.third + i) % P_RING

    @block.sync
    def _(sp):
        sp.dma_start(wq[:, :, :], io["wq"].rearrange("(g p) n -> p g n", p=P)).then_inc(const_in, 16)

        def load_x(G):
            wait(sp, q_done, G.n)
            sp.dma_start(x_proj[:, :, :], x_d[G.batch]).then_inc(x_in, 16)
            wait(sp, q_masked, G.n)
            sp.dma_start(mask_cols[:, :],
                         io["mask"][bass.ds(G.batch, 1), :].partition_broadcast(P)).then_inc(mask_in, 16)

        def stack(G):
            made_at, read_at = early(sp, G.n + 1), early(sp, TILES * (G.n - 2))
            wait(sp, score_done, read_at)
            for part, made, places in (
                (q_hi, hi_made, ((keys1, 0), (qrys1, 0), (qrys1, 1), (keys1, 2), (qrys1, 3), (keys2, 0))),
                (q_mid, mid_made, ((keys1, 1), (qrys1, 2), (keys2, 1), (qrys2, 1))),
                (q_lo, lo_made, ((keys1, 3), (qrys2, 0))),
            ):
                sp.wait_ge(made, made_at)
                for buffers, quarter in places:
                    sp.dma_start(buffers[G.third][DK * quarter:DK * quarter + DK, :, :],
                                 part[:, :]).then_inc(stacked, 16)
            for buffers, row in ((keys2, "dead"), (qrys2, "live")):
                sp.dma_start(buffers[G.third][MASK_AT:MASK_AT + 1, :, :],
                             io[row][bass.ds(G.batch, 1), :].rearrange("o (h t) -> o h t", h=1)
                             .to_broadcast([1, HG, T])).then_inc(stacked, 16)

        def place_max(G):
            for part, made, at in ((max_hi, maxhi_made, MAX_AT), (max_lo, maxlo_made, MAX_AT + 1)):
                sp.wait_ge(made, G.n + 1)
                sp.dma_start(qrys2[G.third][at:at + 1, :, :], part[:, :]).then_inc(max_in, 16)

        def stage(G):
            after, projected = G.shift(1), G.shift(2)
            if projected.exists and projected.half == 0:
                load_x(projected)
            done = finished(after)
            if done and done.exists:
                wait(sp, final_done, 2 * done.batch)
                sp.dma_start(x_res[:, :, :], x_d[done.batch]).then_inc(xres_in, 16)
            if G.is_at(-2):
                sp.dma_start(ident[:, :], io["ident"]).then_inc(const_in, 16)
                sp.dma_start(wo[:, :, :], io["wo"].rearrange("(g p) n -> p g n", p=P)).then_inc(const_in, 16)
                sp.wait_ge(mrow_out, 32)
                sp.wait_ge(ones_made, 1 + len(keys2))
            if G.is_at(2):
                sp.dma_start(wih[:, :, :], io["wih"].rearrange("(k p) n -> p k n", p=P)).then_inc(w_in, 16)
            if projected.exists:
                stack(projected)
            if after.exists:
                place_max(after)

        staged(sp, stage)

    @block.gpsimd
    def _(pool):
        for buf in keys2:
            pool.memset(buf[MAX_AT:MAX_AT + DK, :, :], -1.0).then_inc(ones_made, 1)
        pool.wait_ge(ones_made, len(keys2))
        pool.memset(ones[:, :], 1.0).then_inc(ones_made, 1)
        pool.dma_start(mask_rows, io["mask"]).then_inc(mrow_in, 16)
        pool.wait_ge(live_made, 1)
        pool.dma_start(io["live"], live[:, :]).then_inc(mrow_out, 16)
        pool.wait_ge(dead_made, 2)
        pool.dma_start(io["dead"], dead[:, :]).then_inc(mrow_out, 16)

        def stage(G):
            projected = G.shift(2)
            if projected.exists:
                pool.wait_ge(mid_made, projected.n + 1)
                wait(pool, stacked, STACKED * projected.n)
                pool.tensor_tensor(q_lo[:, :], q_live[:, :], q_mid[:, :], ALU.subtract).then_inc(lo_made, 1)
            if G.exists:
                for i in range(1, KT):
                    for h in range(HG):
                        if i == 1 and h == 0:
                            wait(pool, total_done, G.n)
                        if i > 1:
                            pool.wait_ge(added, ADDS * G.n + HG * (i - 2) + h + 1)
                        pool.wait_ge(probs_made, TILES * G.n + HG * i + h + 1)
                        so_far = probs[:, place(G, 0), h, :] if i == 1 else total[:, h, :]
                        pool.tensor_tensor(total[:, h, :], so_far, probs[:, place(G, i), h, :],
                                           ALU.add).then_inc(added, 1)

        staged(pool, stage)

    @block.scalar
    def _(act):
        def project(G):
            act.wait_ge(q_masked, G.n + 1)
            wait(act, v_turned, G.n)
            act.activation(q_all[:, :], small[:, :], ACT.Copy).then_inc(q_copied, 1)

        def values(G):
            act.wait_ge(v_turned, G.n + 1)
            wait(act, round_done, KT * (G.n - 2))
            act.activation(vals[G.third][:, :, :].rearrange("p a c -> p (a c)"), small[:, :],
                           ACT.Copy).then_inc(v_copied, 1)

        def finish(batch, half):
            act.wait_ge(final_done, 2 * batch + half + 1)
            act.activation(xT[:, 2 * half:2 * half + 2, :, bass.ds(batch, 1)].rearrange("p k t o -> p k (t o)"),
                           final[:, :].rearrange("p (k t) -> p k t", k=2), ACT.Copy).then_inc(final_used, 1)

        def take_context(G):
            wait(act, context_made, G.n)
            act.wait_ge(round_done, KT * (G.n + 1))
            act.activation(raw[:, :], pv[:, :], ACT.Copy).then_inc(raw_copied, 1)

        def stage(G):
            before, projected, done = G.shift(-1), G.shift(2), finished(G)
            for i in range(KT):
                for h in range(HG):
                    if G.exists:
                        if h == 0:
                            wait(act, round_done, KT * G.n + i - P_RING + 1)
                            if i >= P_RING:
                                act.wait_ge(added, ADDS * G.n + READ_BY[i - P_RING])
                            elif before.exists:
                                act.wait_ge(added, ADDS * before.n + READ_BY[i - P_RING + KT])
                        act.wait_ge(score_done, TILES * G.n + HG * i + h + 1)
                        act.activation(probs[:, place(G, i), h, :], score[h % 2][:, :], ACT.Exp,
                                       scale=SCALE).then_inc(probs_made, 1)
                    if (i, h) == (1, 0) and before.exists:
                        take_context(before)
                    if (i, h) == (1, 1) and projected.exists:
                        project(projected)
                    if (i, h) == (2, 1) and projected.exists:
                        values(projected)
                    if i >= 2 and h == 2 and done and done.exists:
                        finish(done.batch, i - 2)

        staged(act, stage)

    @block.vector
    def _(dve):
        dve.wait_ge(mrow_in, 16)
        dve.tensor_copy(live[:, :], mask_rows).then_inc(live_made, 1)
        dve.tensor_scalar(mask_rows, mask_rows, -1.0, None, ALU.add).then_inc(dead_made, 1)
        dve.wait_ge(dead_made, 1)
        dve.tensor_scalar(dead[:, :], mask_rows, BIG, None, ALU.mult).then_inc(dead_made, 1)

        def project(G):
            n = G.n
            dve.wait_ge(mask_in, 16 * (G.batch + 1))
            wait(dve, lo_made, n)
            dve.wait_ge(q_done, n + 1)
            dve.tensor_tensor(q_live[:, :], small[:, :], mask_cols[:, :], ALU.mult).then_inc(q_masked, 1)
            wait(dve, stacked, STACKED * n)
            dve.wait_ge(q_masked, n + 1)
            dve.tensor_copy(q_hi[:, :], q_live[:, :]).then_inc(hi_made, 1)
            dve.wait_ge(hi_made, n + 1)
            dve.tensor_tensor(q_live[:, :], q_live[:, :], q_hi[:, :], ALU.subtract).then_inc(rest_made, 1)
            dve.wait_ge(rest_made, n + 1)
            dve.tensor_copy(q_mid[:, :], q_live[:, :]).then_inc(mid_made, 1)

        def maxima(G, first, last):
            if first == 0:
                wait(dve, max_turned, G.n)
            for s in range(first, last):
                at = s % HG * KT + s // HG
                dve.wait_ge(peek_done, TILES * G.n + s + 1)
                dve.tensor_reduce(row_max[:, at:at + 1], peek[s % 2][:, :], AX.X, ALU.max).then_inc(peek_used, 1)

        def split_max(G):
            wait(dve, max_in, PLACED * G.n)
            dve.wait_ge(max_turned, G.n + 1)
            dve.tensor_copy(max_hi[:, :], small[0:HG * KT, 0:P]).then_inc(maxhi_made, 1)
            dve.wait_ge(maxhi_made, G.n + 1)
            dve.tensor_tensor(max_lo[:, :], small[0:HG * KT, 0:P], max_hi[:, :],
                              ALU.subtract).then_inc(maxlo_made, 1)

        def normalise(G):
            wait(dve, context_made, G.n)
            dve.wait_ge(total_done, G.n + 1)
            dve.reciprocal(inv_sum[:, :], psum_p[:, :]).then_inc(inv_made, 1)
            wait(dve, final_done, 2 * G.batch)
            dve.wait_ge(raw_copied, G.n + 1)
            dve.wait_ge(inv_made, G.n + 1)
            dve.tensor_tensor(context[G.half][:, :], raw[:, :], inv_sum[:, :], ALU.mult).then_inc(context_made, 1)

        def stage(G):
            before, after, projected = G.shift(-1), G.shift(1), G.shift(2)
            for i in range(KT):
                if after.exists:
                    maxima(after, PEEKS[HG * i], PEEKS[HG * i + HG])
                if i == 0 and projected.exists:
                    project(projected)
            if after.exists:
                split_max(after)
            if before.exists:
                normalise(before)

        staged(dve, stage)

    @block.tensor
    def _(pe):
        pe.wait_ge(const_in, 48)
        pe.wait_ge(ones_made, 1 + len(keys2))

        def project(G):
            pe.wait_ge(x_in, 16 * (G.batch + 1))
            wait(pe, v_copied, G.n)
            wait(pe, maxlo_made, G.n - 1)
            for k in range(NG):
                mm = pe.matmul(small[:, :], wq[:, k, P * G.half:P * G.half + P], x_proj[:, k, :],
                               start=(k == 0), stop=(k == NG - 1))
            mm.then_inc(q_done, 1)

        def peeks(G, first, last):
            if first == 0 and last > 0:
                pe.wait_ge(stacked, STACKED * (G.n + 1))
            for s in range(first, last):
                i, h = s // HG, s % HG
                wait(pe, peek_used, TILES * G.n + s - 1)
                pe.matmul(peek[s % 2][:, :], keys1[G.third][:, h, P * i:P * i + P], qrys1[G.third][:, h, :],
                          start=True, stop=True).then_inc(peek_done, 1)

        def turn_max(G):
            pe.wait_ge(peek_used, TILES * (G.n + 1))
            pe.wait_ge(v_copied, min(G.n + 2, GROUPS) if isinstance(G.n, int) else G.n + 2)
            pe.transpose(small[0:HG * KT, 0:P], row_max[:, :], ident[:, :]).then_inc(max_turned, 1)

        def turn_values(G):
            pe.wait_ge(q_copied, G.n + 1)
            for a in range(KT):
                mm = pe.transpose(small[:, P * a:P * a + P], q_all[:, P * a:P * a + P], ident[:, :])
            mm.then_inc(v_turned, 1)

        def score_tile(G, i, h):
            wait(pe, probs_made, TILES * G.n + HG * i + h - 1)
            pe.matmul(score[h % 2][:, :], keys1[G.third][:, h, P * i:P * i + P], qrys1[G.third][:, h, :],
                      start=True, stop=False)
            if i == 0 and h == 0:
                pe.wait_ge(max_in, PLACED * (G.n + 1))
            pe.matmul(score[h % 2][:, :], keys2[G.third][0:PASS2, h, P * i:P * i + P],
                      qrys2[G.third][0:PASS2, h, :], start=False, stop=True).then_inc(score_done, 1)

        def weigh(G, i):
            if i == 0:
                wait(pe, raw_copied, G.n)
                pe.wait_ge(v_copied, G.n + 1)
            pe.wait_ge(probs_made, TILES * G.n + HG * (i + 1))
            for h in range(HG):
                mm = pe.matmul(pv[DK * h:DK * h + DK, :], vals[G.third][:, i, h:P:HG], probs[:, place(G, i), h, :],
                               start=(i == 0), stop=(i == KT - 1))
            mm.then_inc(round_done, 1)

        def sum_up(G):
            wait(pe, inv_made, G.n)
            pe.wait_ge(added, ADDS * (G.n + 1))
            for h in range(HG):
                mm = pe.matmul(psum_p[DK * h:DK * h + DK, :], ones[:, :], total[:, h, :], start=True, stop=True)
            mm.then_inc(total_done, 1)

        def finish(G, half):
            if half == 0:
                pe.wait_ge(xres_in, 16 * (G.batch + 1))
                pe.wait_ge(context_made, G.n + 1)
            wait(pe, final_used, 2 * G.batch + half)
            for kk in range(2):
                k = 2 * half + kk
                at = D * kk
                for g in range(NG):
                    pe.matmul(final[:, at + P * g:at + P * g + P], x_res[:, g, P * k:P * k + P], ident[:, :],
                              start=(kk == 0 and g == 0), stop=False, is_transpose=True, skip_group_check=True)
                for g in range(NG):
                    mm = pe.matmul(final[:, at:at + D], context[g][:, P * k:P * k + P],
                                   wo[:, g, :], start=False, stop=(g == NG - 1), skip_group_check=True)
            mm.then_inc(final_done, 1)

        def stage(G):
            before, after, projected, done = G.shift(-1), G.shift(1), G.shift(2), finished(G)
            for i in range(KT):
                for h in range(HG):
                    if G.exists:
                        score_tile(G, i, h)
                    if after.exists:
                        peeks(after, PEEKS[HG * i + h], PEEKS[HG * i + h + 1])
                    if (i, h) == (1, 1) and before.exists:
                        sum_up(before)
                if i == 0 and projected.exists:
                    project(projected)
                if i == 0 and before.exists:
                    weigh(before, KT - 1)
                if i == 1 and projected.exists:
                    turn_values(projected)
                if i >= 1 and G.exists:
                    weigh(G, i - 1)
                if i == 2:
                    if after.exists:
                        turn_max(after)
                if i in (1, 2) and done and done.exists:
                    finish(done, i - 1)

        staged(pe, stage)


def gru(nc, ctx, io, xT, ident, wih, w_in):
    def sb(name, shape, dt=F32):
        return ctx.enter_context(nc.sbuf_tensor(name, shape, dt))

    def ps(name):
        return ctx.enter_context(nc.psum_tensor(name, [P, 512], F32))

    def sem(name):
        return ctx.enter_context(nc.semaphore(name))

    whh = sb("whh", [P, KF, KF, GATES * P])
    bias_i = sb("bias_i", [P, GATES * KF])
    bias_h = sb("bias_h", [P, GATES * KF])
    bias_row = sb("bias_row", [P, T])
    spread = sb("spread", [P, B])
    state = [sb(f"state_{c}", [P, KF, CH, B]) for c in range(2)]
    cond = sb("cond", [P, P])
    xc = [sb(f"xc_{c}", [P, KF, CB]) for c in range(2)]
    gi = [sb(f"gi_{c}", [P, GATES, KF, CH, B]) for c in range(2)]
    sum_r, sum_n, sum_z = sb("sum_r", [P, P]), sb("sum_n", [P, P]), sb("sum_z", [P, P])
    cond_turned = sb("cond_turned", [P, P])
    r_pre, r_gate, rhn, n_pre, n_gate, z_pre, z_gate, diff, zdiff = (
        sb(name, [P, KF, B]) for name in ("r_pre", "r_gate", "rhn", "n_pre", "n_gate",
                                          "z_pre", "z_gate", "diff", "zdiff"))
    y = sb("y", [P, KF, CB])
    y_rows = sb("y_rows", [P, T])

    rn = ps("rn")
    z = ps("z")
    gi_sum = [ps(f"gi_sum_{q}") for q in range(GATES)]
    y_turned = ps("y_turned")

    whh_in = sem("whh_in")
    b_in, cond_in, b_made, zeroed, psum_zeroed = (sem("b_in"), sem("cond_in"), sem("b_made"), sem("zeroed"),
                                                  sem("psum_zeroed"))
    h0_turned, state_made = sem("h0_turned"), sem("state_made")
    xc_made, gi_summed, gi_made = sem("xc_made"), sem("gi_summed"), sem("gi_made")
    rn_done, z_done, r_turned, n_turned, z_turned = (
        sem("rn_done"), sem("z_done"), sem("r_turned"), sem("n_turned"), sem("z_turned"))
    row_zeroed, row_in, spread_made = sem("row_zeroed"), sem("row_in"), sem("spread_made")
    rpre_made, r_made, rhn_made, npre_made, n_made = (
        sem("rpre_made"), sem("r_made"), sem("rhn_made"), sem("npre_made"), sem("n_made"))
    zpre_made, z_made, diff_made, zdiff_made = sem("zpre_made"), sem("z_made"), sem("diff_made"), sem("zdiff_made")
    y_made, y_done, y_copied, y_out = sem("y_made"), sem("y_done"), sem("y_copied"), sem("y_out")

    out_d = io["out"].rearrange("b t f -> t b f")

    block = ctx.enter_context(nc.Block())

    def chunked(eng, chunk):
        chunk(0, 0)
        chunk(1, 1)
        with eng.Fori(1, CHUNKS // 2 - 1) as pair:
            chunk(2 * pair, 0)
            chunk(2 * pair + 1, 1)
        chunk(CHUNKS - 2, 0)
        chunk(CHUNKS - 1, 1)

    def is_first(c):
        return isinstance(c, int) and c == 0

    def is_last(c):
        return isinstance(c, int) and c == CHUNKS - 1

    def batches(sums):
        return sums[:, :].rearrange("p (k b) -> p k b", k=KF)[:, :, 0:B]

    def old_state(side, s):
        if s:
            return state[side][:, :, s - 1, :]
        return state[1 - side][:, :, CH - 1, :]

    @block.sync
    def _(sp):
        sp.dma_start(bias_i[:, :], io["b_ih"]).then_inc(b_in, 16)
        sp.wait_ge(row_zeroed, 1)
        sp.dma_start(bias_row[0:1, :], io["b_n"]).then_inc(row_in, 16)
        sp.dma_start(bias_h[:, :], io["b_hh"]).then_inc(b_in, 16)
        sp.dma_start(whh[:, :, :, :],
                     io["whh"].rearrange("(k p) (j n) -> p k j n", p=P, j=KF)).then_inc(whh_in, 16)

        def chunk(c, side):
            sp.wait_ge(y_copied, c + 1)
            sp.dma_start(out_d[bass.ds(c * CH, CH), :, :], y_rows[:, :]).then_inc(y_out, 16)
        chunked(sp, chunk)
        sp.wait_ge(y_out, 16 * CHUNKS)

    @block.gpsimd
    def _(pool):
        pool.memset(cond[:, :], 0.0).then_inc(zeroed, 1)
        pool.wait_ge(zeroed, 1)
        def fetch(c, side):
            pool.tensor_copy(xc[side][:, :, :].rearrange("p k (t b) -> p k t b", t=CH),
                             xT[:, :, bass.ds(c * CH, CH), :]).then_inc(xc_made, 1)

        fetch(0, 0)
        fetch(1, 1)
        for k in range(KF):
            pool.dma_start(cond[DK * k:DK * k + B, :],
                           io["mask"].rearrange("b (k j u) -> b k j u", k=KF, j=KF)[:, :, k, :]).then_inc(cond_in, 16)

        def chunk(c, side):
            if not isinstance(c, int) or c + 2 < CHUNKS:
                pool.wait_ge(gi_made, GATES * (c + 1))
                fetch(c + 2, side)
            pool.wait_ge(state_made, c * CH + CH + 1)
            wait(pool, y_done, c)
            pool.tensor_tensor(y[:, :, :].rearrange("p k (s b) -> p k s b", s=CH), state[side][:, :, :, :],
                               xT[:, :, bass.ds(c * CH, CH), :], ALU.add).then_inc(y_made, 1)
        chunked(pool, chunk)

    @block.scalar
    def _(act):
        def copy_y(c):
            act.wait_ge(y_done, c + 1)
            wait(act, y_out, 16 * c)
            act.activation(y_rows[:, :], y_turned[:, :], ACT.Copy).then_inc(y_copied, 1)

        def chunk(c, side):
            for s in range(CH):
                t = c * CH + s
                act.wait_ge(rpre_made, t + 1)
                act.activation(r_gate[:, :, :], r_pre[:, :, :], ACT.Sigmoid).then_inc(r_made, 1)
                act.wait_ge(npre_made, t + 1)
                act.activation(n_gate[:, :, :], n_pre[:, :, :], ACT.Tanh).then_inc(n_made, 1)
                act.wait_ge(zpre_made, t + 1)
                act.activation(z_gate[:, :, :], z_pre[:, :, :], ACT.Sigmoid).then_inc(z_made, 1)
                if s == KF and not is_first(c):
                    copy_y(c - 1)
        chunked(act, chunk)
        copy_y(CHUNKS - 1)

    @block.vector
    def _(dve):
        dve.memset(bias_row[:, :], 0.0).then_inc(row_zeroed, 1)
        dve.memset(spread[:, :], 0.0).then_inc(spread_made, 1)
        dve.memset(rn[:, :], 0.0).then_inc(psum_zeroed, 1)
        dve.memset(z[:, :], 0.0).then_inc(psum_zeroed, 1)
        dve.wait_ge(spread_made, 1)
        dve.memset(spread[0:1, :], 1.0).then_inc(spread_made, 1)
        dve.wait_ge(b_in, 32)
        dve.tensor_tensor(bias_i[:, 0:2 * KF], bias_i[:, 0:2 * KF], bias_h[:, 0:2 * KF],
                          ALU.add).then_inc(b_made, 1)
        dve.wait_ge(cond_in, 16 * KF)
        dve.transpose(cond_turned[:, :], cond[:, :]).then_inc(h0_turned, 1)
        dve.wait_ge(h0_turned, 1)
        dve.tensor_copy(state[1][:, :, CH - 1, :], batches(cond_turned)).then_inc(state_made, 1)
        dve.wait_ge(b_made, 1)

        def bias(vec, q, shape):
            return vec[:, KF * q:KF * q + KF].rearrange("p (k o) -> p k o", o=1).to_broadcast(shape)

        def gates(c, side, q):
            dve.wait_ge(gi_summed, GATES * c + q + 1)
            dve.tensor_tensor(gi[side][:, q, :, :, :].rearrange("p k s b -> p k (s b)"),
                              gi_sum[q][:, :].rearrange("p (k n) -> p k n", k=KF),
                              bias(bias_i, q, [P, KF, CB]), ALU.add).then_inc(gi_made, 1)

        for q in range(GATES):
            gates(0, 0, q)

        def chunk(c, side):
            for s in range(CH):
                t = c * CH + s
                if s == 0:
                    dve.wait_ge(gi_made, GATES * c + GATES)
                    if not isinstance(c, int) or c >= 2:
                        dve.wait_ge(y_made, c - 1)
                dve.wait_ge(rn_done, t + 1)
                dve.transpose(sum_r[:, :], rn[:, 0:P]).then_inc(r_turned, 1)
                dve.wait_ge(r_turned, t + 1)
                dve.tensor_tensor(r_pre[:, :, :], batches(sum_r), gi[side][:, 0, :, s, :],
                                  ALU.add).then_inc(rpre_made, 1)
                dve.transpose(sum_n[:, :], rn[:, P:2 * P]).then_inc(n_turned, 1)
                dve.wait_ge(n_turned, t + 1)
                dve.wait_ge(r_made, t + 1)
                dve.tensor_tensor(rhn[:, :, :], r_gate[:, :, :], batches(sum_n), ALU.mult).then_inc(rhn_made, 1)
                dve.wait_ge(z_done, t + 1)
                dve.transpose(sum_z[:, :], z[:, 0:P]).then_inc(z_turned, 1)
                dve.wait_ge(rhn_made, t + 1)
                dve.tensor_tensor(n_pre[:, :, :], rhn[:, :, :], gi[side][:, 2, :, s, :],
                                  ALU.add).then_inc(npre_made, 1)
                dve.wait_ge(z_turned, t + 1)
                dve.tensor_tensor(z_pre[:, :, :], batches(sum_z), gi[side][:, 1, :, s, :],
                                  ALU.add).then_inc(zpre_made, 1)
                dve.wait_ge(n_made, t + 1)
                dve.tensor_tensor(diff[:, :, :], old_state(side, s), n_gate[:, :, :],
                                  ALU.subtract).then_inc(diff_made, 1)
                dve.wait_ge(diff_made, t + 1)
                dve.wait_ge(z_made, t + 1)
                dve.tensor_tensor(zdiff[:, :, :], z_gate[:, :, :], diff[:, :, :], ALU.mult).then_inc(zdiff_made, 1)
                dve.wait_ge(zdiff_made, t + 1)
                dve.tensor_tensor(state[side][:, :, s, :], n_gate[:, :, :], zdiff[:, :, :],
                                  ALU.add).then_inc(state_made, 1)
                if s in EVAC and not is_last(c):
                    gates(c + 1, 1 - side, EVAC.index(s))
        chunked(dve, chunk)

    @block.tensor
    def _(pe):
        pe.wait_ge(w_in, 16)
        pe.wait_ge(psum_zeroed, 2)

        def gate_sums(c, side, first, last):
            for f in range(first, min(last, GATES * KF * KF)):
                q, m, k = f // (KF * KF), f // KF % KF, f % KF
                if f == 0:
                    pe.wait_ge(xc_made, c + 1)
                if m == 0 and k == 0:
                    wait(pe, gi_made, GATES * (c - 1) + q + 1)
                at = T * q + P * m
                mm = pe.matmul(gi_sum[q][:, P * m:P * m + P], wih[:, k, at:at + P], xc[side][:, k, :],
                               start=(k == 0), stop=(k == KF - 1))
                if m == KF - 1 and k == KF - 1:
                    mm.then_inc(gi_summed, 1)

        def turn_y(c, k):
            if k == 0:
                pe.wait_ge(y_made, c + 1)
                wait(pe, y_copied, c)
            mm = pe.transpose(y_turned[:, P * k:P * k + P], y[:, k, :], ident[:, :])
            if k == KF - 1:
                mm.then_inc(y_done, 1)

        gate_sums(0, 0, 0, GATES * KF * KF)
        pe.wait_ge(whh_in, 16)
        pe.wait_ge(row_in, 16)
        pe.wait_ge(spread_made, 2)

        def start_n(t):
            wait(pe, n_turned, t)
            for j in range(KF):
                pe.matmul(rn[DK * j:DK * j + B, P:2 * P], spread[:, :], bias_row[:, P * j:P * j + P],
                          start=True, stop=False, skip_group_check=True)

        def recur(sums, side, s, k, first, last, started=False):
            for j in range(KF):
                mm = pe.matmul(sums[DK * j:DK * j + B, 0:last - first], old_state(side, s)[:, k, :],
                               whh[:, k, j, first:last], start=(k == 0 and not started), stop=(k == KF - 1),
                               skip_group_check=started)
            return mm

        def chunk(c, side):
            for s in range(CH):
                t = c * CH + s
                done = FILL * s
                pe.wait_ge(state_made, t + 1)
                for k in range(KF):
                    mm = recur(rn, side, s, k, 0, 2 * P, started=True)
                mm.then_inc(rn_done, 1)
                for k in range(KF):
                    mm = recur(z, side, s, k, 2 * P, 3 * P)
                mm.then_inc(z_done, 1)
                if s < CH - 1 or not is_last(c):
                    start_n(t + 1)
                if 1 <= s <= KF and not is_first(c):
                    turn_y(c - 1, s - 1)
                if not is_last(c):
                    gate_sums(c + 1, 1 - side, done, done + FILL)
        start_n(0)
        chunked(pe, chunk)
        for k in range(KF):
            turn_y(CHUNKS - 1, k)


def build(nc, io):
    with ExitStack() as ctx:
        xT = ctx.enter_context(nc.sbuf_tensor("xT", [P, KF, D, B], F32))
        ident = ctx.enter_context(nc.sbuf_tensor("ident", [P, P], F32))
        wih = ctx.enter_context(nc.sbuf_tensor("wih", [P, KF, GATES * T], F32))
        w_in = ctx.enter_context(nc.semaphore("w_in"))
        with ExitStack() as inner:
            attention(nc, inner, io, xT, ident, wih, w_in)
        with ExitStack() as inner:
            gru(nc, inner, io, xT, ident, wih, w_in)


def kernel(x, cond_2048, L0_cond_Wq, L0_cond_Wo, L1_cond_W_ih, L1_cond_W_hh, L1_cond_b_ih, L1_cond_b_hh):
    import numpy as np
    import concourse.bacc as bacc
    from concourse.bass_utils import run_bass_kernel_spmd

    w_hh = np.asarray(L1_cond_W_hh).reshape(T, GATES, KF, KF, DK)[:, [0, 2, 1]]
    arrays = {
        "x": x,
        "mask": cond_2048,
        "wq": np.asarray(L0_cond_Wq).T.reshape(D, NG, HG, DK).transpose(0, 1, 3, 2).reshape(D, D),
        "wo": np.asarray(L0_cond_Wo).T,
        "wih": L1_cond_W_ih,
        "whh": w_hh.transpose(0, 3, 1, 2, 4).reshape(T, GATES * T),
        "b_ih": np.asarray(L1_cond_b_ih).reshape(GATES * KF, P).T,
        "b_hh": np.asarray(L1_cond_b_hh).reshape(GATES * KF, P).T,
        "b_n": np.asarray(L1_cond_b_hh).reshape(GATES, KF, KF, DK)[2].transpose(1, 0, 2).reshape(1, T),
        "ident": np.eye(P, dtype=np.float32),
    }
    arrays = {name: np.ascontiguousarray(a) for name, a in arrays.items()}
    nc = bacc.Bacc("TRN2", target_bir_lowering=False, num_devices=1)
    io = {name: nc.dram_tensor("in_" + name, a.shape, F32, kind="ExternalInput").ap() for name, a in arrays.items()}
    io["out"] = nc.dram_tensor("out_0", (B, D, T), F32, kind="ExternalOutput").ap()
    io["live"] = nc.dram_tensor("live_rows", (B, T), BF16, kind="Internal").ap()
    io["dead"] = nc.dram_tensor("dead_rows", (B, T), BF16, kind="Internal").ap()
    build(nc, io)
    result = run_bass_kernel_spmd(nc, [{"in_" + name: a for name, a in arrays.items()}], core_ids=[0])
    return result.results[0]["out_0"]
```
